# Optimizing a Trainium2 kernel written in Bass

```python
import numpy as np
import jax
import jax.numpy as jnp

def _softmax(x, axis=-1):
    return jax.nn.softmax(x, axis=axis)

def _gelu(x):
    return jax.nn.gelu(x, approximate=True)

def _silu(x):
    return jax.nn.silu(x)

def _sigmoid(x):
    return jax.nn.sigmoid(x)

def _layernorm(x, axis=-1, eps=1e-05):
    m = jnp.mean(x, axis=axis, keepdims=True)
    v = jnp.var(x, axis=axis, keepdims=True)
    return (x - m) / jnp.sqrt(v + eps)

def _scatter_add(tgt, idx, src, axis=0):
    return tgt.at[idx].add(src)

def _segment_sum(src, seg, n):
    return jax.ops.segment_sum(src, seg, n)
kernel_name = 'mk_early_fusion_embed_d1_tok_img256_r4_1a4d02'

def setup_inputs(seed: int=0):
    np.random.seed(seed)
    _w = jnp.asarray

    def _rec_inputs():
        import jax
        import jax.numpy as jnp
        _rk = jax.random.key(seed)
        x = -0.00016672 + 0.999947 * jax.random.normal(jax.random.fold_in(_rk, 1), (16, 3, 64, 64), jnp.float32)
        x_txt = jax.random.randint(jax.random.fold_in(_rk, 51), (16, 128), 0, 64, jnp.int32)
        itok_BS_0_255 = jax.random.randint(jax.random.fold_in(_rk, 71), (16, 128), 0, 64, jnp.int32)
        itok_BS_0_511 = jax.random.randint(jax.random.fold_in(_rk, 72), (16, 128), 0, 128, jnp.int32)
        itok_BS_0_127 = jax.random.randint(jax.random.fold_in(_rk, 73), (16, 128), 0, 128, jnp.int32)
        itok_BS_0_63 = jax.random.randint(jax.random.fold_in(_rk, 74), (16, 128), 0, 64, jnp.int32)
        itok_BS_0_3 = jax.random.randint(jax.random.fold_in(_rk, 75), (16, 128), 0, 4, jnp.int32)
        return (x, x_txt, itok_BS_0_255, itok_BS_0_511, itok_BS_0_127, itok_BS_0_63, itok_BS_0_3)
    x, x_txt, itok_BS_0_255, itok_BS_0_511, itok_BS_0_127, itok_BS_0_63, itok_BS_0_3 = _rec_inputs()

    def _L0_tok_setup():
        import jax, jax.numpy as jnp
        import numpy as np
        PATCH = 16
        key = jax.random.key(seed)
        k1, k2, k3 = jax.random.split(key, 3)
        B, C, H, Wd = (64, 3, 96, 96)
        E = 64
        pdim = PATCH * PATCH * C
        x = jax.random.normal(k1, (B, C, H, Wd), dtype=jnp.float32)
        W = jax.random.normal(k2, (E, pdim), dtype=jnp.float32) * pdim ** (-0.5)
        b = jax.random.normal(k3, (E,), dtype=jnp.float32) * 0.01
        return {'x': x, 'W': W, 'b': b}
    _L0_tok_all = _L0_tok_setup()
    _L0_tok_in = {k: v for k, v in _L0_tok_all.items() if k in ('W', 'b')}
    del _L0_tok_all

    def _L0_txt_setup():
        import jax, jax.numpy as jnp
        import numpy as np
        B, S = (128, 512)
        D_OUT = 64
        EMB = 16
        EPS_W = 1e-08
        EPS_LN = 1e-05

        def ternary_linear(x, W, b):
            scale = jnp.mean(jnp.abs(W))
            w_q = jnp.clip(jnp.round(W / (scale + EPS_W)), -1.0, 1.0) * scale
            w_eff = W + jax.lax.stop_gradient(w_q - W)
            return jnp.einsum('bsk,ok->bso', x, w_eff) + b

        def layer_norm(x, gamma, beta):
            mu = jnp.mean(x, axis=-1, keepdims=True)
            var = jnp.mean(jnp.square(x - mu), axis=-1, keepdims=True)
            return (x - mu) * jax.lax.rsqrt(var + EPS_LN) * gamma + beta
        key = jax.random.key(seed)
        ks = jax.random.split(key, 16)
        vocabs = {'event_type': 64, 'fault_class': 64, 'syscall_class': 128, 'opcode_family': 128, 'transition_type': 64, 'result_class': 4}
        inp = {}
        for i, (name, v) in enumerate(vocabs.items()):
            inp[name] = jax.random.randint(ks[i], (B, S), 0, v, dtype=jnp.int64)
        inp['E_et'] = jax.random.normal(ks[6], (64, EMB), dtype=jnp.float32)
        inp['E_fc'] = jax.random.normal(ks[7], (64, EMB), dtype=jnp.float32)
        inp['E_sc'] = jax.random.normal(ks[8], (128, EMB), dtype=jnp.float32)
        inp['E_of'] = jax.random.normal(ks[9], (128, EMB), dtype=jnp.float32)
        inp['E_tt'] = jax.random.normal(ks[10], (64, EMB), dtype=jnp.float32)
        inp['E_rc'] = jax.random.normal(ks[11], (4, EMB), dtype=jnp.float32)
        inp['W'] = jax.random.normal(ks[12], (D_OUT, 96), dtype=jnp.float32) * 0.1
        inp['b'] = jnp.zeros((D_OUT,), dtype=jnp.float32)
        inp['gamma'] = jnp.ones((D_OUT,), dtype=jnp.float32)
        inp['beta'] = jnp.zeros((D_OUT,), dtype=jnp.float32)
        return inp
    _L0_txt_all = _L0_txt_setup()
    _L0_txt_in = {k: v for k, v in _L0_txt_all.items() if k in ('E_et', 'E_fc', 'E_sc', 'E_of', 'E_tt', 'E_rc', 'W', 'b', 'gamma', 'beta')}
    del _L0_txt_all

    def _L0_attn_setup():
        import jax, jax.numpy as jnp
        import numpy as np
        HEADS = 8
        EPS = 1e-05

        def _ln(t, w, b, headc):
            m = jnp.mean(t, axis=-1, keepdims=True)
            d = t - m
            std = jnp.sqrt(jnp.sum(d * d, axis=-1, keepdims=True) / (headc - 1))
            return w * (d / (std + EPS)) + b
        key = jax.random.key(seed)
        B, N, C = (32, 1024, 64)
        headc = C // HEADS
        x = jax.random.normal(key, (B, N, C), dtype=jnp.float32)
        return {'x': x, 'kln_weight': jnp.ones((HEADS, 1, headc), dtype=jnp.float32), 'kln_bias': jnp.zeros((HEADS, 1, headc), dtype=jnp.float32), 'vln_weight': jnp.ones((HEADS, 1, headc), dtype=jnp.float32), 'vln_bias': jnp.zeros((HEADS, 1, headc), dtype=jnp.float32)}
    _L0_attn_all = _L0_attn_setup()
    _L0_attn_in = {k: v for k, v in _L0_attn_all.items() if k in ('kln_weight', 'kln_bias', 'vln_weight', 'vln_bias')}
    del _L0_attn_all

    def _L0_ffn_setup():
        import jax, jax.numpy as jnp
        import numpy as np
        DIM = 64
        HEADS = 8
        NUM_KEYS = 64
        NUM_KV = NUM_KEYS ** 2
        PK_TOPK = 16
        FINAL_TOPK = 16
        DIM_KEY = DIM // 2
        P = 2

        def _pk(x, Wq_pk, pk_keys):
            b, n, _ = x.shape
            q = (x @ Wq_pk).reshape(b, n, P, HEADS, DIM_KEY).transpose(2, 0, 1, 3, 4)
            sim = jnp.einsum('pbnhd,pkhd->pbnhk', q, pk_keys)
            scores, idx = jax.lax.top_k(sim, PK_TOPK)
            idx0 = idx[0]
            idx1 = idx[1] * NUM_KEYS
            index = (idx0[..., :, None] + idx1[..., None, :]).reshape(b, n, HEADS, PK_TOPK * PK_TOPK)
            score = (scores[0][..., :, None] + scores[1][..., None, :]).reshape(b, n, HEADS, PK_TOPK * PK_TOPK)
            final_scores, pk_idx = jax.lax.top_k(score, FINAL_TOPK)
            final_indices = jnp.take_along_axis(index, pk_idx, axis=-1)
            final_scores = jax.nn.softmax(final_scores, axis=-1)
            return (final_scores, final_indices)
        key = jax.random.key(seed)
        ks = jax.random.split(key, 7)
        b, n = (2, 256)
        std = 0.02
        x = jax.random.normal(ks[0], (b, n, DIM), dtype=jnp.float32)
        Wq_pk = jax.random.normal(ks[1], (DIM, P * HEADS * DIM_KEY), dtype=jnp.float32) * std
        pk_keys = jax.random.normal(ks[2], (P, NUM_KEYS, HEADS, DIM_KEY), dtype=jnp.float32) * std
        Wq = jax.random.normal(ks[3], (DIM, HEADS * DIM), dtype=jnp.float32) * std
        keys_table = jax.random.normal(ks[4], (NUM_KV * HEADS, DIM), dtype=jnp.float32) * std
        values_table = jax.random.normal(ks[5], (NUM_KV * HEADS, DIM), dtype=jnp.float32) * std
        Wo = jax.random.normal(ks[6], (DIM * HEADS, DIM), dtype=jnp.float32) * std
        return {'x': x, 'Wq_pk': Wq_pk, 'pk_keys': pk_keys, 'Wq': Wq, 'keys_table': keys_table, 'values_table': values_table, 'Wo': Wo}
    _L0_ffn_all = _L0_ffn_setup()
    _L0_ffn_in = {k: v for k, v in _L0_ffn_all.items() if k in ('Wq_pk', 'pk_keys', 'Wq', 'keys_table', 'values_table', 'Wo')}
    del _L0_ffn_all
    return {'x': x, 'x_txt': x_txt, 'itok_BS_0_255': itok_BS_0_255, 'itok_BS_0_511': itok_BS_0_511, 'itok_BS_0_127': itok_BS_0_127, 'itok_BS_0_63': itok_BS_0_63, 'itok_BS_0_3': itok_BS_0_3, 'L0_tok_W': _L0_tok_in['W'], 'L0_tok_b': _L0_tok_in['b'], 'L0_txt_E_et': _L0_txt_in['E_et'], 'L0_txt_E_fc': _L0_txt_in['E_fc'], 'L0_txt_E_sc': _L0_txt_in['E_sc'], 'L0_txt_E_of': _L0_txt_in['E_of'], 'L0_txt_E_tt': _L0_txt_in['E_tt'], 'L0_txt_E_rc': _L0_txt_in['E_rc'], 'L0_txt_W': _L0_txt_in['W'], 'L0_txt_b': _L0_txt_in['b'], 'L0_txt_gamma': _L0_txt_in['gamma'], 'L0_txt_beta': _L0_txt_in['beta'], 'L0_attn_kln_weight': _L0_attn_in['kln_weight'], 'L0_attn_kln_bias': _L0_attn_in['kln_bias'], 'L0_attn_vln_weight': _L0_attn_in['vln_weight'], 'L0_attn_vln_bias': _L0_attn_in['vln_bias'], 'L0_ffn_Wq_pk': _L0_ffn_in['Wq_pk'], 'L0_ffn_pk_keys': _L0_ffn_in['pk_keys'], 'L0_ffn_Wq': _L0_ffn_in['Wq'], 'L0_ffn_keys_table': _L0_ffn_in['keys_table'], 'L0_ffn_values_table': _L0_ffn_in['values_table'], 'L0_ffn_Wo': _L0_ffn_in['Wo']}

def reference(x, x_txt, itok_BS_0_255, itok_BS_0_511, itok_BS_0_127, itok_BS_0_63, itok_BS_0_3, L0_tok_W, L0_tok_b, L0_txt_E_et, L0_txt_E_fc, L0_txt_E_sc, L0_txt_E_of, L0_txt_E_tt, L0_txt_E_rc, L0_txt_W, L0_txt_b, L0_txt_gamma, L0_txt_beta, L0_attn_kln_weight, L0_attn_kln_bias, L0_attn_vln_weight, L0_attn_vln_bias, L0_ffn_Wq_pk, L0_ffn_pk_keys, L0_ffn_Wq, L0_ffn_keys_table, L0_ffn_values_table, L0_ffn_Wo):
    import jax
    import jax.numpy as jnp

    def _L0_tok_ref(x, W, b):
        import jax, jax.numpy as jnp
        import numpy as np
        PATCH = 16
        B, C, H, Wd = x.shape
        p = PATCH
        nH, nW = (H // p, Wd // p)
        patches = x.reshape(B, C, nH, p, nW, p)
        patches = patches.transpose(0, 2, 4, 1, 3, 5)
        patches = patches.reshape(B, nH * nW, C * p * p)
        return jnp.einsum('bnk,ek->bne', patches, W) + b

    def _L0_txt_ref(event_type, fault_class, syscall_class, opcode_family, transition_type, result_class, E_et, E_fc, E_sc, E_of, E_tt, E_rc, W, b, gamma, beta):
        import jax, jax.numpy as jnp
        import numpy as np
        B, S = (128, 512)
        D_OUT = 64
        EMB = 16
        EPS_W = 1e-08
        EPS_LN = 1e-05

        def ternary_linear(x, W, b):
            scale = jnp.mean(jnp.abs(W))
            w_q = jnp.clip(jnp.round(W / (scale + EPS_W)), -1.0, 1.0) * scale
            w_eff = W + jax.lax.stop_gradient(w_q - W)
            return jnp.einsum('bsk,ok->bso', x, w_eff) + b

        def layer_norm(x, gamma, beta):
            mu = jnp.mean(x, axis=-1, keepdims=True)
            var = jnp.mean(jnp.square(x - mu), axis=-1, keepdims=True)
            return (x - mu) * jax.lax.rsqrt(var + EPS_LN) * gamma + beta
        combined = jnp.concatenate([E_et[event_type], E_fc[fault_class], E_sc[syscall_class], E_of[opcode_family], E_tt[transition_type], E_rc[result_class]], axis=-1)
        z = ternary_linear(combined, W, b)
        return layer_norm(z, gamma, beta)

    def _L0_attn_ref(x, kln_weight, kln_bias, vln_weight, vln_bias):
        import jax, jax.numpy as jnp
        import numpy as np
        HEADS = 8
        EPS = 1e-05

        def _ln(t, w, b, headc):
            m = jnp.mean(t, axis=-1, keepdims=True)
            d = t - m
            std = jnp.sqrt(jnp.sum(d * d, axis=-1, keepdims=True) / (headc - 1))
            return w * (d / (std + EPS)) + b
        B, N, C = x.shape
        headc = C // HEADS
        qkv = x.reshape(B, N, HEADS, headc).transpose(0, 2, 1, 3)
        k = _ln(qkv, kln_weight, kln_bias, headc)
        v = _ln(qkv, vln_weight, vln_bias, headc)
        kv = jnp.einsum('bhnd,bhne->bhde', k, v) / N
        out = jnp.einsum('bhnd,bhde->bhne', qkv, kv)
        out = out.transpose(0, 2, 1, 3).reshape(B, N, C)
        return out + x

    def _L0_ffn_ref(x, Wq_pk, pk_keys, Wq, keys_table, values_table, Wo):
        import jax, jax.numpy as jnp
        import numpy as np
        DIM = 64
        HEADS = 8
        NUM_KEYS = 64
        NUM_KV = NUM_KEYS ** 2
        PK_TOPK = 16
        FINAL_TOPK = 16
        DIM_KEY = DIM // 2
        P = 2

        def _pk(x, Wq_pk, pk_keys):
            b, n, _ = x.shape
            q = (x @ Wq_pk).reshape(b, n, P, HEADS, DIM_KEY).transpose(2, 0, 1, 3, 4)
            sim = jnp.einsum('pbnhd,pkhd->pbnhk', q, pk_keys)
            scores, idx = jax.lax.top_k(sim, PK_TOPK)
            idx0 = idx[0]
            idx1 = idx[1] * NUM_KEYS
            index = (idx0[..., :, None] + idx1[..., None, :]).reshape(b, n, HEADS, PK_TOPK * PK_TOPK)
            score = (scores[0][..., :, None] + scores[1][..., None, :]).reshape(b, n, HEADS, PK_TOPK * PK_TOPK)
            final_scores, pk_idx = jax.lax.top_k(score, FINAL_TOPK)
            final_indices = jnp.take_along_axis(index, pk_idx, axis=-1)
            final_scores = jax.nn.softmax(final_scores, axis=-1)
            return (final_scores, final_indices)
        b, n, d = x.shape
        q = (x @ Wq).reshape(b, n, HEADS, DIM) * DIM ** (-0.5)
        kv_scores, indices = _pk(x, Wq_pk, pk_keys)
        offsets = jnp.arange(HEADS, dtype=indices.dtype) * NUM_KV
        ind = indices + offsets[None, None, :, None]
        k = jnp.einsum('bnhk,bnhkd->bnhd', kv_scores, keys_table[ind])
        v = jnp.einsum('bnhk,bnhkd->bnhd', kv_scores, values_table[ind])
        sim = jnp.einsum('bihd,bjhd->bhij', q, k)
        neg = -jnp.finfo(sim.dtype).max
        causal = jnp.tril(jnp.ones((n, n), dtype=bool))
        sim = jnp.where(causal, sim, neg)
        attn = jax.nn.softmax(sim, axis=-1)
        out = jnp.einsum('bhij,bjhd->bhid', attn, v)
        out = out.transpose(0, 2, 1, 3).reshape(b, n, HEADS * DIM)
        return out @ Wo
    h = _L0_tok_ref(x, L0_tok_W, L0_tok_b)
    h = jnp.concatenate([h, _L0_txt_ref(x_txt, itok_BS_0_255, itok_BS_0_511, itok_BS_0_127, itok_BS_0_63, itok_BS_0_3, L0_txt_E_et, L0_txt_E_fc, L0_txt_E_sc, L0_txt_E_of, L0_txt_E_tt, L0_txt_E_rc, L0_txt_W, L0_txt_b, L0_txt_gamma, L0_txt_beta)], axis=1)
    h = h + _L0_attn_ref(_layernorm(h, axis=-1), L0_attn_kln_weight, L0_attn_kln_bias, L0_attn_vln_weight, L0_attn_vln_bias)
    h = h + _L0_ffn_ref(_layernorm(h, axis=-1), L0_ffn_Wq_pk, L0_ffn_pk_keys, L0_ffn_Wq, L0_ffn_keys_table, L0_ffn_values_table, L0_ffn_Wo)
    return h

_drawn_inputs = setup_inputs


def setup_inputs(seed=0):
    import zlib

    import numpy as np

    out = dict(_drawn_inputs(seed))
    spreads = {'L0_txt_b': (0.0, 0.1),
     'L0_txt_gamma': (1.0, 0.2),
     'L0_txt_beta': (0.0, 0.1),
     'L0_attn_kln_weight': (1.0, 0.2),
     'L0_attn_kln_bias': (0.0, 0.301),
     'L0_attn_vln_weight': (1.0, 0.2),
     'L0_attn_vln_bias': (0.0, 0.1)}
    factors = {'L0_tok_b': 8.0,
     'L0_ffn_Wq_pk': 41.968,
     'L0_ffn_pk_keys': 40.11,
     'L0_ffn_Wq': 64.0,
     'L0_ffn_keys_table': 64.0,
     'L0_ffn_values_table': 40.43,
     'L0_ffn_Wo': 40.316}
    for name, (base, spread) in spreads.items():
        noise = np.random.default_rng([zlib.crc32(name.encode()), seed]).standard_normal(out[name].shape)
        drawn = base * np.exp(spread * noise) if base else spread * noise
        out[name] = jnp.asarray(drawn.astype(out[name].dtype))
    for name, factor in factors.items():
        out[name] = (out[name] * factor).astype(out[name].dtype)
    return out
```

```python
import concourse.bass as bass
from concourse import mybir
from contextlib import ExitStack

F32 = mybir.dt.float32
I32 = mybir.dt.int32
U32 = mybir.dt.uint32
ALU = mybir.AluOpType
ACT = mybir.ActivationFunctionType
X = mybir.AxisListType.X

P = 128
D = 64
HEADS = 8
HC = D // HEADS
BATCH = 16
PATCHES = 16
SEQ = PATCHES + P
GROUP = P // PATCHES
ROUNDS = BATCH // GROUP
PER_ROUND = 1 + GROUP
TILES = ROUNDS * PER_ROUND
KPATCH = 3 * 16 * 16 // P
VCHUNKS = 4
EMB = 96
NK = 64
TOP = 16
KD = D // 2
SLOTS = 4
NEG = -3.0e38
DROPPED = -3.4028235e38
MAGIC = 12582912.0

BLOCKS = [(0, 1, 16), (1, 1, 8), (2, 2, 5), (4, 4, 3), (8, 8, 1)]
CAND = sum(rows * cols for _, rows, cols in BLOCKS)


def build(nc, patches, tok_w, tok_b, tokens, tables, txt_w, vectors, pk_w, pk_keys, q_w, kv_table, o_w, out):
    with ExitStack() as ctx:
        def sb(name, shape, dt=F32):
            return ctx.enter_context(nc.sbuf_tensor(name, shape, dt))

        def sem(name):
            return ctx.enter_context(nc.semaphore(name))

        patches_sb = sb("patches_sb", [P, KPATCH, ROUNDS * P])
        tok_w_sb = sb("tok_w_sb", [P, KPATCH, D])
        tok_b_sb = sb("tok_b_sb", [P, D])
        tokens_sb = sb("tokens_sb", [P, VCHUNKS, BATCH * P], I32)
        onehot = sb("onehot", [P, VCHUNKS, BATCH * P])
        tables_sb = sb("tables_sb", [EMB, VCHUNKS, P])
        txt_w_sb = sb("txt_w_sb", [EMB, D])
        w_eff = sb("w_eff", [EMB, D])
        w_stat = sb("w_stat", [EMB, 4])
        projected = sb("projected", [P, VCHUNKS, D])
        vec_sb = sb("vec_sb", [P, 7, D])
        pk_w_sb = sb("pk_w_sb", [KD, 2 * HEADS, D])
        pk_keys_sb = sb("pk_keys_sb", [KD, 2 * HEADS, NK])
        pk_fold = sb("pk_fold", [D, HEADS * 2 * NK])
        q_w_sb = sb("q_w_sb", [D, HEADS * D])
        o_w_sb = sb("o_w_sb", [P, 4, D])

        ones = sb("ones", [P, P])
        ident = sb("ident", [P, P])
        vocab_i = sb("vocab_i", [P, 2], I32)
        vocab_f = sb("vocab_f", [P, 2])
        place_i = sb("place_i", [P, CAND], I32)
        place_f = sb("place_f", [P, CAND])
        batch_of_row = sb("batch_of_row", [P, GROUP])
        head_blocks = sb("head_blocks", [D, D])
        patch_mask = sb("patch_mask", [P, P])
        text_mask = sb("text_mask", [P, 2 * P])
        batch_window = sb("batch_window", [P, 2 * P - PATCHES])
        eps = sb("eps", [P, 1])

        h = sb("h", [P, TILES, D])
        x1 = sb("x1", [P, TILES, D])
        dev = sb("dev", [P, TILES, D])
        sq = sb("sq", [P, TILES, D])
        x2 = sb("x2", [P, TILES, D])
        k1 = sb("k1", [P, TILES, D])
        v1 = sb("v1", [P, TILES, D])
        v1_split = sb("v1_split", [P, ROUNDS, GROUP, D])
        mean = sb("mean", [P, TILES * HEADS])
        var = sb("var", [P, TILES * HEADS])
        std = sb("std", [P, TILES * HEADS])
        kv1 = sb("kv1", [D, ROUNDS, GROUP, D])
        patch_out_t = sb("patch_out_t", [D, ROUNDS, P])
        x1_t = sb("x1_t", [D, TILES * P])
        x2_t = sb("x2_t", [D, (TILES + 1) * P])

        x2_t_next = sb("x2_t_next", [D, P])
        scores = sb("scores", [P, HEADS, 2, NK])
        rest = sb("rest", [P, 2, NK])
        half_top = sb("half_top", [P, 2, TOP])
        half_idx = sb("half_idx", [P, 2, TOP], U32)
        half_key = sb("half_key", [P, 2, TOP])
        cand = sb("cand", [P, CAND])
        cand_row = sb("cand_row", [P, CAND])
        cand_rest = sb("cand_rest", [P, CAND])
        best_at = sb("best_at", [P, TOP], U32)
        best_place = sb("best_place", [P, TOP])
        picked = sb("picked", [P, TOP, CAND])
        picked_row = sb("picked_row", [P, TOP, CAND])
        best_row = sb("best_row", [P, TOP])
        best = sb("best", [P, HEADS, TOP])
        neg_best = sb("neg_best", [P, HEADS])
        rows = sb("rows", [P, HEADS, TOP], I32)
        weight = sb("weight", [P, HEADS, TOP])
        weight_sum = sb("weight_sum", [P, HEADS])
        weight_inv = sb("weight_inv", [P, HEADS])
        weight_n = sb("weight_n", [P, TOP])
        gathered = onehot[:, :, :].rearrange("p s (k c) -> p s k c", c=P)
        part = sb("part", [P, 4, P])
        half_sum = sb("half_sum", [P, 2, P])
        kv_patch = sb("kv_patch", [P, 2, HEADS, D])
        kv_text = sb("kv_text", [P, 2, HEADS, D])
        q_t = sb("q_t", [P, 4, P])
        k_t_patch = sb("k_t_patch", [P, 4, P])
        k_t_text = sb("k_t_text", [P, 4, P])
        masked = sb("masked", [P, 2, 2 * P])
        neg_max = sb("neg_max", [P, HEADS])
        prob = sb("prob", [P, 2, 2 * P])
        prob_sum = sb("prob_sum", [P, HEADS])
        prob_inv = sb("prob_inv", [P, HEADS])
        prob_t = sb("prob_t", [P, 2, 2 * P])
        attended = sb("attended", [P, HEADS * D])
        attended_t = sb("attended_t", [P, 4, P])
        y = sb("y", [P, D])

        bank = [ctx.enter_context(nc.psum_tensor(f"bank{i}", [P, 512], F32)) for i in range(8)]

        patch_loaded = sem("patch_loaded")
        txt_w_loaded = sem("txt_w_loaded")
        tokens_loaded = sem("tokens_loaded")
        vec_loaded = sem("vec_loaded")
        pk_loaded = sem("pk_loaded")
        late_loaded = sem("late_loaded")
        consts_made = sem("consts_made")
        w_summed = sem("w_summed")
        w_total = sem("w_total")
        w_made = sem("w_made")
        fold_done = sem("fold_done")
        fold_copied = sem("fold_copied")
        tables_done = sem("tables_done")
        tables_copied = sem("tables_copied")
        onehot_made = sem("onehot_made")
        patch_embedded = sem("patch_embedded")
        text_embedded = sem("text_embedded")
        var_ready = sem("var_ready")
        std_ready = sem("std_ready")
        x1_ready = sem("x1_ready")
        x1_t_done = sem("x1_t_done")
        x1_t_copied = sem("x1_t_copied")
        kv1_in = sem("kv1_in")
        kv1_done = sem("kv1_done")
        kv1_ready = sem("kv1_ready")
        lin_text_done = sem("lin_text_done")
        lin_patch_t_done = sem("lin_patch_t_done")
        lin_patch_t_copied = sem("lin_patch_t_copied")
        lin_patch_done = sem("lin_patch_done")
        x2_ready = sem("x2_ready")
        x2_t_done = sem("x2_t_done")
        x2_t_copied = sem("x2_t_copied")

        x2_next_ready = sem("x2_next_ready")
        scores_done = sem("scores_done")
        scores_copied = sem("scores_copied")
        scores_used = sem("scores_used")
        best_ready = sem("best_ready")
        weight_ready = sem("weight_ready")
        rows_ready = sem("rows_ready")
        searches_begun = sem("searches_begun")
        gathers_begun = sem("gathers_begun")
        slot_free = sem("slot_free")
        slot_filled = [sem(f"slot_filled{s}") for s in range(SLOTS)]
        kv_ready = sem("kv_ready")
        q_done = sem("q_done")
        q_copied = sem("q_copied")
        k_t_done = sem("k_t_done")
        k_t_copied = sem("k_t_copied")
        sim_done = sem("sim_done")
        sim_masked = sem("sim_masked")
        prob_ready = sem("prob_ready")
        prob_t_done = sem("prob_t_done")
        prob_t_copied = sem("prob_t_copied")
        av_done = sem("av_done")
        av_scaled = sem("av_scaled")
        at_t_done = sem("at_t_done")
        at_t_copied = sem("at_t_copied")
        y_done = sem("y_done")
        y_ready = sem("y_ready")
        y_stored = sem("y_stored")
        y_free = sem("y_free")

        sim = [bank[4], bank[7]]
        turned = [bank[5], bank[2]]

        block = ctx.enter_context(nc.Block())

        VEC = {name: i for i, name in enumerate(["b", "gamma", "beta", "k_w", "k_b", "v_w", "v_b"])}

        def vec(name, n):
            return vec_sb[:, VEC[name]:VEC[name] + 1, :].to_broadcast([P, n, D])

        def over(stat, shape):
            return stat.unsqueeze(len(shape) - 1).to_broadcast(shape)

        GROUPS_OF_4 = (TILES + 3) // 4

        def copy_transposed(act, dst, done, copied):
            for g in range(GROUPS_OF_4):
                n = min(4, TILES - 4 * g) * P
                act.wait_ge(done, g + 1)
                nc.scalar.copy(dst[:, 4 * g * P:4 * g * P + n], bank[5 + g % 2][0:D, 0:n]).then_inc(copied, 1)

        def wait_apart(eng, semaphore, value, passed):
            eng.wait_ge(semaphore, value)
            eng.sem_inc(passed, 1)

        @block.sync
        def _(sp):
            sp.dma_start(txt_w_sb[:, :], txt_w).then_inc(txt_w_loaded, 16)
            sp.dma_start(tables_sb[:, :, :], tables).then_inc(txt_w_loaded, 16)
            half = P // 2
            for kind, (low, high, chunk) in enumerate([(0, half, 0), (half, P, 0), (0, P, 1), (0, P, 2),
                                                       (0, half, 3), (half, P, 3)]):
                sp.dma_start(tokens_sb[low:high, chunk, :],
                             tokens[kind:kind + 1, :].partition_broadcast(high - low)).then_inc(tokens_loaded, 16)
            sp.dma_start(pk_w_sb[:, :, :], pk_w).then_inc(pk_loaded, 16)
            sp.dma_start(pk_keys_sb[:, :, :], pk_keys).then_inc(pk_loaded, 16)
            sp.dma_start(q_w_sb[:, :], q_w).then_inc(late_loaded, 16)
            sp.dma_start(o_w_sb[:, :, :], o_w).then_inc(late_loaded, 16)

            def store(tile, at):
                sp.wait_ge(y_ready, tile + 1)
                sp.dma_start(out[at, :], y[:, :]).then_inc(y_stored, 16)
                sp.wait_ge(y_stored, (tile + 1) * 16)
                sp.sem_inc(y_free, 1)

            with nc.Fori(0, ROUNDS, engines=[sp.engine]) as r:
                store(r * PER_ROUND, bass.ds(r * PER_ROUND * P, P))
                with nc.Fori(0, GROUP, engines=[sp.engine]) as b:
                    store(r * PER_ROUND + 1 + b, bass.ds((r * PER_ROUND + 1 + b) * P, P))
            sp.wait_ge(y_stored, 16 * TILES)

        @block.gpsimd
        def _(pool):
            nc.gpsimd.memset(ones[:, :], 1.0)
            nc.gpsimd.memset(ident[:, :], 0.0)
            nc.gpsimd.memset(eps[:, :], 1e-5)
            nc.gpsimd.memset(batch_of_row[:, :], 1.0)
            nc.gpsimd.memset(head_blocks[:, :], 1.0 / SEQ)
            nc.gpsimd.memset(patch_mask[:, :], 0.0)
            nc.gpsimd.memset(text_mask[:, :], 0.0)
            nc.gpsimd.memset(batch_window[:, :], NEG)
            nc.gpsimd.memset(x2_t[:, TILES * P:], 0.0)
            nc.gpsimd.iota(vocab_i[:, 0:1], pattern=[[0, 1]], base=0, channel_multiplier=1)
            nc.gpsimd.iota(vocab_i[:, 1:2], pattern=[[0, 1]], base=0, channel_multiplier=1)
            nc.gpsimd.iota(place_i[:, :], pattern=[[1, CAND]], base=0, channel_multiplier=0)
            pool.drain()
            nc.gpsimd.iota(vocab_i[P // 2:, 1:2], pattern=[[0, 1]], base=0, channel_multiplier=1)
            pool.drain()
            nc.gpsimd.memset(batch_window[:, P - PATCHES:P], 0.0)
            nc.gpsimd.affine_select(out=ident[:, :], in_=ident[:, :], compare_op=ALU.not_equal, fill=1.0,
                                    base=0, pattern=[[-1, P]], channel_multiplier=1)

            def keep_block(t, width, fill, per):
                n = t.shape[1] // per
                v = t.rearrange("p (n c) -> p n c", c=per)
                for base, sign in ((0, 1), (width - 1, -1)):
                    nc.gpsimd.affine_select(out=v, in_=v, compare_op=ALU.is_ge, fill=fill, base=base,
                                            pattern=[[-sign * width, n], [0, per]], channel_multiplier=sign)
                    pool.drain()

            keep_block(batch_of_row[:, :], PATCHES, 0.0, 1)
            keep_block(head_blocks[:, :], HC, 0.0, HC)
            keep_block(patch_mask[:, :], PATCHES, NEG, PATCHES)
            for t in (patch_mask[:, :], text_mask[:, P:]):
                nc.gpsimd.affine_select(out=t, in_=t, compare_op=ALU.is_ge, fill=NEG,
                                        base=0, pattern=[[-1, P]], channel_multiplier=1)
            nc.gpsimd.tensor_copy(place_f[:, :], place_i[:, :])
            pool.drain()
            nc.gpsimd.tensor_copy(vocab_f[:, :], vocab_i[:, :]).then_inc(consts_made, 1)

            def gather(tile, head):
                slot = head % SLOTS
                pool.wait_ge(slot_free, tile * HEADS + head + 1)
                wait_apart(pool, rows_ready, tile * HEADS + head + 1, gathers_begun)
                for k in range(TOP):
                    nc.gpsimd.indirect_dma_start(
                        gathered[:, slot, k, :], None, kv_table,
                        bass.IndirectOffsetOnAxis(rows[:, head, k:k + 1], 0)).then_inc(slot_filled[slot], 16)

            with nc.Fori(0, TILES, engines=[pool.engine]) as tile:
                for head in range(HEADS):
                    gather(tile, head)

        @block.scalar
        def _(act):
            act.dma_start(patches_sb[:, :, :], patches).then_inc(patch_loaded, 16)
            act.dma_start(tok_w_sb[:, :, :], tok_w).then_inc(patch_loaded, 16)
            act.dma_start(tok_b_sb[:, :], tok_b.partition_broadcast(P)).then_inc(patch_loaded, 16)
            act.dma_start(vec_sb[:, :, :].rearrange("p a d -> p (a d)"),
                          vectors.partition_broadcast(P)).then_inc(vec_loaded, 16)

            for i in range(2):
                act.wait_ge(fold_done, i + 1)
                nc.scalar.copy(pk_fold[:, i * 512:(i + 1) * 512], bank[i][0:D, :]).then_inc(fold_copied, 1)
            act.wait_ge(tables_done, 1)
            nc.scalar.copy(projected[:, :, :].rearrange("p c d -> p (c d)"),
                           bank[2][:, 0:VCHUNKS * D]).then_inc(tables_copied, 1)

            act.wait_ge(consts_made, 1)
            for i, (n, scale, bias) in enumerate([(BATCH, 1.0 / D, eps[:, :]), (TILES, 1.0 / D, eps[:, :]),
                                                  (TILES * HEADS, 1.0 / (HC - 1), 0.0), (TILES, 1.0 / D, eps[:, :])]):
                if i == 3:
                    copy_transposed(act, x1_t, x1_t_done, x1_t_copied)
                    act.wait_ge(lin_patch_t_done, 1)
                    nc.scalar.copy(patch_out_t[:, :, :].rearrange("p a b -> p (a b)"),
                                   bank[0][0:D, 0:ROUNDS * P]).then_inc(lin_patch_t_copied, 1)
                act.wait_ge(var_ready, i + 1)
                nc.scalar.activation(std[:, 0:n], var[:, 0:n], ACT.Sqrt, scale=scale, bias=bias).then_inc(std_ready, 1)
            copy_transposed(act, x2_t, x2_t_done, x2_t_copied)
            act.wait_ge(x2_t_copied, GROUPS_OF_4)

            def copy_scores(tile, first):
                act.wait_ge(consts_made, 1)
                if not first:
                    act.wait_ge(scores_done, tile)
                nc.scalar.copy(x2_t_next[:, :], x2_t[:, bass.ds(tile * P, P)]).then_inc(x2_next_ready, 1)
                if not first:
                    act.wait_ge(scores_used, tile)
                act.wait_ge(scores_done, tile + 1)
                flat = scores[:, :, :, :].rearrange("p h s k -> p (h s k)")
                nc.scalar.copy(flat[:, 0:512], bank[0][:, :])
                nc.scalar.copy(flat[:, 512:1024], bank[1][:, :]).then_inc(scores_copied, 1)

            def weigh(tile, head):
                act.wait_ge(best_ready, tile * HEADS + head + 1)
                nc.scalar.activation(weight[:, head, :], best[:, head, :], ACT.Exp, bias=neg_best[:, head:head + 1],
                                     accum_out=weight_sum[:, head:head + 1]).then_inc(weight_ready, 1)

            copy_scores(0, True)
            for head in range(HEADS):
                weigh(0, head)

            def tile_step(tile, text):
                copy_scores(tile + 1, False)
                act.wait_ge(q_done, tile + 1)
                nc.scalar.mul(q_t[:, :, :].rearrange("p a b -> p (a b)"), bank[2][:, :], D ** -0.5).then_inc(q_copied, 1)
                for head in range(HEADS):
                    weigh(tile + 1, head)
                k_t = k_t_text if text else k_t_patch
                width = 2 * P if text else P
                act.wait_ge(k_t_done, tile + 1)
                nc.scalar.copy(k_t[:, :, :].rearrange("p a b -> p (a b)"), bank[3][:, :]).then_inc(k_t_copied, 1)
                for i in range(HEADS + 1):
                    if i < HEADS:
                        act.wait_ge(sim_masked, tile * HEADS + i + 1)
                        nc.scalar.activation(prob[:, i % 2, 0:width], masked[:, i % 2, 0:width], ACT.Exp,
                                             bias=neg_max[:, i:i + 1],
                                             accum_out=prob_sum[:, i:i + 1]).then_inc(prob_ready, 1)
                    if i >= 1:
                        head = i - 1
                        if head >= 2:
                            act.wait_ge(av_done, tile * HEADS + head - 1)
                        act.wait_ge(prob_t_done, tile * HEADS + head + 1)
                        nc.scalar.copy(prob_t[:, head % 2, 0:width],
                                       turned[head % 2][:, 0:width]).then_inc(prob_t_copied, 1)
                act.wait_ge(at_t_done, tile + 1)
                nc.scalar.copy(attended_t[:, :, :].rearrange("p a b -> p (a b)"), bank[3][:, :]).then_inc(at_t_copied, 1)

            with nc.Fori(0, ROUNDS, engines=[act.engine]) as r:
                tile_step(r * PER_ROUND, False)
                with nc.Fori(0, GROUP, engines=[act.engine]) as b:
                    tile_step(r * PER_ROUND + 1 + b, True)

        @block.tensor
        def _(pe):
            mm = nc.tensor.matmul
            pe.wait_ge(pk_loaded, 32)
            for half in range(2):
                for i in range(HEADS):
                    u = half * HEADS + i
                    last = mm(bank[half][0:D, i * NK:(i + 1) * NK], pk_w_sb[:, u, :], pk_keys_sb[:, u, :],
                              start=True, stop=True)
                last.then_inc(fold_done, 1)
            pe.wait_ge(consts_made, 1)
            pe.wait_ge(w_summed, 1)
            mm(bank[3][0:EMB, 0:1], ones[0:EMB, 0:EMB], w_stat[:, 0:1], start=True, stop=True).then_inc(w_total, 1)
            pe.wait_ge(patch_loaded, 48)
            for r in range(ROUNDS):
                for c in range(KPATCH):
                    last = mm(bank[4][:, r * D:(r + 1) * D], patches_sb[:, c, r * P:(r + 1) * P],
                              tok_w_sb[:, c, :], start=(c == 0), stop=(c == KPATCH - 1))
            last.then_inc(patch_embedded, 1)
            pe.wait_ge(txt_w_loaded, 32)
            pe.wait_ge(w_made, 1)
            for c in range(VCHUNKS):
                last = mm(bank[2][:, c * D:(c + 1) * D], tables_sb[:, c, :], w_eff[:, :], start=True, stop=True)
            last.then_inc(tables_done, 1)
            pe.wait_ge(tables_copied, 1)
            pe.wait_ge(fold_copied, 2)
            pe.wait_ge(onehot_made, VCHUNKS)
            for b in range(BATCH):
                o = bank[b // GROUP][:, (b % GROUP) * D:(b % GROUP + 1) * D]
                for c in range(VCHUNKS):
                    last = mm(o, onehot[:, c, b * P:(b + 1) * P], projected[:, c, :],
                              start=(c == 0), stop=(c == VCHUNKS - 1))
                if b % GROUP == GROUP - 1:
                    last.then_inc(text_embedded, 1)

            def transpose_tiles(src, done, copied):
                for g in range(GROUPS_OF_4):
                    if g >= 2:
                        pe.wait_ge(copied, g - 1)
                    for i in range(min(4, TILES - 4 * g)):
                        last = nc.tensor.transpose(bank[5 + g % 2][0:D, i * P:(i + 1) * P],
                                                   src[:, 4 * g + i, :], ident[:, :])
                    last.then_inc(done, 1)

            pe.wait_ge(x1_ready, 1)
            transpose_tiles(x1, x1_t_done, x1_t_copied)
            pe.wait_ge(kv1_in, 1)
            for r in range(ROUNDS):
                t = r * PER_ROUND
                mm(bank[3 + r][0:D, :], k1[:, t, :], v1_split[:, r, :, :].rearrange("p b d -> p (b d)"),
                   start=True, stop=False, skip_group_check=True)
                for b in range(GROUP):
                    last = mm(bank[3 + r][0:D, b * D:(b + 1) * D], k1[:, t + 1 + b, :], v1[:, t + 1 + b, :],
                              start=False, stop=(b == GROUP - 1), skip_group_check=True)
                last.then_inc(kv1_done, 1)
            pe.wait_ge(kv1_ready, ROUNDS)
            pe.wait_ge(x1_t_copied, GROUPS_OF_4)
            for r in range(ROUNDS):
                for b in range(GROUP):
                    last = mm(bank[0][0:D, r * P + b * PATCHES:r * P + (b + 1) * PATCHES], kv1[:, r, b, :],
                              x1_t[:, r * PER_ROUND * P + b * PATCHES:r * PER_ROUND * P + (b + 1) * PATCHES],
                              start=True, stop=True)
            last.then_inc(lin_patch_t_done, 1)
            for r in range(ROUNDS):
                for b in range(GROUP):
                    t = r * PER_ROUND + 1 + b
                    last = mm(bank[1 + r][:, b * D:(b + 1) * D], x1_t[:, t * P:(t + 1) * P], kv1[:, r, b, :],
                              start=True, stop=True)
                last.then_inc(lin_text_done, 1)
            pe.wait_ge(lin_patch_t_copied, 1)
            for r in range(ROUNDS):
                last = nc.tensor.transpose(bank[7][:, r * D:(r + 1) * D], patch_out_t[:, r, :], ident[0:D, 0:D])
            last.then_inc(lin_patch_done, 1)
            pe.wait_ge(x2_ready, 1)
            transpose_tiles(x2, x2_t_done, x2_t_copied)
            pe.wait_ge(x2_t_copied, GROUPS_OF_4)
            pe.wait_ge(late_loaded, 32)

            def score(tile, first):
                if not first:
                    pe.wait_ge(scores_copied, tile)
                pe.wait_ge(x2_next_ready, tile + 1)
                for i in range(2):
                    last = mm(bank[i][:, :], x2_t_next[:, :], pk_fold[:, i * 512:(i + 1) * 512], start=True, stop=True)
                last.then_inc(scores_done, 1)

            score(0, True)

            def tile_step(tile, text):
                score(tile + 1, False)
                for j in range(4):
                    last = mm(bank[2][:, j * P:(j + 1) * P], q_w_sb[:, j * P:(j + 1) * P],
                              x2_t[:, bass.ds(tile * P, P)], start=True, stop=True)
                last.then_inc(q_done, 1)
                kv, k_t = (kv_text, k_t_text) if text else (kv_patch, k_t_patch)
                pe.wait_ge(kv_ready, tile + 1)
                for j in range(4):
                    last = nc.tensor.transpose(bank[3][:, j * P:(j + 1) * P],
                                               kv[:, 0, 2 * j:2 * j + 2, :].rearrange("p a d -> p (a d)"), ident[:, :])
                last.then_inc(k_t_done, 1)
                pe.wait_ge(q_copied, tile + 1)
                pe.wait_ge(k_t_copied, tile + 1)
                keys = ([k_t_patch] if text else []) + [k_t]
                vals = ([kv_patch] if text else []) + [kv]
                for i in range(HEADS + 2):
                    if i < HEADS:
                        if i >= 2:
                            pe.wait_ge(sim_masked, tile * HEADS + i - 1)
                        lo = (i % 2) * D
                        for n, key in enumerate(keys):
                            last = mm(sim[i % 2][:, n * P:(n + 1) * P], q_t[lo:lo + D, i // 2, :], key[lo:lo + D, i // 2, :],
                                      start=True, stop=True)
                        last.then_inc(sim_done, 1)
                    if 1 <= i <= HEADS:
                        head = i - 1
                        if head >= 2:
                            pe.wait_ge(prob_t_copied, tile * HEADS + head - 1)
                        pe.wait_ge(prob_ready, tile * HEADS + head + 1)
                        for n in range(len(keys)):
                            last = nc.tensor.transpose(turned[head % 2][:, n * P:(n + 1) * P], prob[:, head % 2, n * P:(n + 1) * P],
                                                       ident[:, :])
                        last.then_inc(prob_t_done, 1)
                    if i >= 2:
                        head = i - 2
                        pe.wait_ge(prob_t_copied, tile * HEADS + head + 1)
                        for n, val in enumerate(vals):
                            last = mm(bank[6][:, head * D:(head + 1) * D], prob_t[:, head % 2, n * P:(n + 1) * P],
                                      val[:, 1, head, :], start=(n == 0), stop=(n == len(vals) - 1))
                        last.then_inc(av_done, 1)
                pe.wait_ge(av_scaled, tile + 1)
                for j in range(4):
                    last = nc.tensor.transpose(bank[3][:, j * P:(j + 1) * P], attended[:, j * P:(j + 1) * P], ident[:, :])
                last.then_inc(at_t_done, 1)
                pe.wait_ge(at_t_copied, tile + 1)
                for j in range(4):
                    last = mm(bank[7][:, 2 * P:2 * P + D], attended_t[:, j, :], o_w_sb[:, j, :], start=(j == 0), stop=(j == 3))
                last.then_inc(y_done, 1)

            with nc.Fori(0, ROUNDS, engines=[pe.engine]) as r:
                tile_step(r * PER_ROUND, False)
                with nc.Fori(0, GROUP, engines=[pe.engine]) as b:
                    tile_step(r * PER_ROUND + 1 + b, True)

        @block.vector
        def _(dve):
            v = nc.vector
            done = dve.drain

            dve.wait_ge(txt_w_loaded, 32)
            v.tensor_reduce(w_stat[:, 0:1], txt_w_sb[:, :], X, ALU.add, apply_absolute_value=True).then_inc(w_summed, 1)
            dve.wait_ge(consts_made, 1)
            dve.wait_ge(tokens_loaded, 6 * 16)
            for c in range(VCHUNKS):
                column = vocab_f[:, 1:2] if c in (0, 3) else vocab_f[:, 0:1]
                v.tensor_scalar(onehot[:, c, :], tokens_sb[:, c, :], column, None, ALU.is_equal).then_inc(onehot_made, 1)
                if c == 0:
                    dve.wait_ge(w_total, 1)
                    v.tensor_scalar(w_stat[:, 1:2], bank[3][0:EMB, 0:1], 1.0 / (EMB * D), None, ALU.mult)
                    done()
                    v.tensor_scalar(w_stat[:, 2:3], w_stat[:, 1:2], 1e-8, None, ALU.add)
                    done()
                    v.reciprocal(w_stat[:, 3:4], w_stat[:, 2:3])
                    done()
                    v.tensor_scalar(w_eff[:, :], txt_w_sb[:, :], w_stat[:, 3:4], None, ALU.mult)
                    done()
                    v.tensor_scalar(w_eff[:, :], w_eff[:, :], 1.0, -1.0, ALU.min, ALU.max)
                    done()
                    v.tensor_scalar(w_eff[:, :], w_eff[:, :], MAGIC, None, ALU.add)
                    done()
                    v.tensor_scalar(w_eff[:, :], w_eff[:, :], MAGIC, None, ALU.subtract)
                    done()
                    v.scalar_tensor_tensor(w_eff[:, :], w_eff[:, :], w_stat[:, 1:2], txt_w_sb[:, :],
                                           ALU.mult, ALU.subtract)
                    done()
                    v.tensor_tensor(w_eff[:, :], w_eff[:, :], txt_w_sb[:, :], ALU.add).then_inc(w_made, 1)

            dve.wait_ge(patch_loaded, 48)
            dve.wait_ge(patch_embedded, 1)
            v.tensor_tensor(h[:, 0:TILES:PER_ROUND, :], bank[4][:, 0:ROUNDS * D].rearrange("p (r d) -> p r d", d=D),
                            tok_b_sb[:, :].unsqueeze(1).to_broadcast([P, ROUNDS, D]), ALU.add)
            dve.wait_ge(vec_loaded, 16)

            def text_tiles(t, r):
                return t[:, r * PER_ROUND + 1:(r + 1) * PER_ROUND, :]

            for r in range(ROUNDS):
                dve.wait_ge(text_embedded, r + 1)
                v.tensor_tensor(text_tiles(h, r), bank[r][:, :].rearrange("p (b d) -> p b d", d=D),
                                vec("b", GROUP), ALU.add)
            done()

            n_std = [0]

            def normalise(parts, groups, width, signal=None):
                at = 0
                for src, cen, squ, _ in parts:
                    n = src.shape[1]
                    v.tensor_reduce(mean[:, at:at + n], src, X, ALU.add)
                    at += n
                done()
                v.tensor_scalar(mean[:, 0:at], mean[:, 0:at], 1.0 / width, None, ALU.mult)
                done()
                at = 0
                for src, cen, squ, _ in parts:
                    n = src.shape[1]
                    v.tensor_tensor(cen, src, over(mean[:, at:at + n], [P, n, width]), ALU.subtract)
                    at += n
                done()
                for src, cen, squ, _ in parts:
                    v.tensor_tensor(squ, cen, cen, ALU.mult)
                done()
                at = 0
                for src, cen, squ, _ in parts:
                    n = src.shape[1]
                    last = v.tensor_reduce(var[:, at:at + n], squ, X, ALU.add)
                    at += n
                last.then_inc(var_ready, 1)
                n_std[0] += 1
                dve.wait_ge(std_ready, n_std[0])
                if groups == "heads":
                    v.tensor_scalar(std[:, 0:at], std[:, 0:at], 1e-5, None, ALU.add)
                    done()
                v.reciprocal(std[:, 0:at], std[:, 0:at])
                done()
                at = 0
                for src, cen, squ, dst in parts:
                    n = src.shape[1]
                    last = v.tensor_tensor(dst, cen, over(std[:, at:at + n], [P, n, width]), ALU.mult)
                    at += n
                if signal is not None:
                    last.then_inc(signal, 1)
                done()

            normalise([tuple(text_tiles(t, r) for t in (h, dev, sq, h)) for r in range(ROUNDS)], "rows", D)
            for name, op in (("gamma", ALU.mult), ("beta", ALU.add)):
                for r in range(ROUNDS):
                    v.tensor_tensor(text_tiles(h, r), text_tiles(h, r), vec(name, GROUP), op)
                done()
            normalise([(h[:, :, :], dev[:, :, :], sq[:, :, :], x1[:, :, :])], "rows", D, x1_ready)
            heads = [t[:, :, :].rearrange("p t (h c) -> p (t h) c", c=HC) for t in (x1, dev, sq, dev)]
            normalise([tuple(heads)], "heads", HC)
            for t, w in ((k1, "k_w"), (v1, "v_w")):
                v.tensor_tensor(t[:, :, :], dev[:, :, :], vec(w, TILES), ALU.mult)
            done()
            for t, w in ((k1, "k_b"), (v1, "v_b")):
                v.tensor_tensor(t[:, :, :], t[:, :, :], vec(w, TILES), ALU.add)
            done()
            for r in range(ROUNDS):
                last = v.tensor_tensor(v1_split[:, r, :, :],
                                       v1[:, r * PER_ROUND:r * PER_ROUND + 1, :].to_broadcast([P, GROUP, D]),
                                       over(batch_of_row[:, :], [P, GROUP, D]), ALU.mult)
            last.then_inc(kv1_in, 1)
            for r in range(ROUNDS):
                dve.wait_ge(kv1_done, r + 1)
                v.tensor_tensor(kv1[:, r, :, :], bank[3 + r][0:D, :].rearrange("p (b d) -> p b d", d=D),
                                head_blocks[:, :].unsqueeze(1).to_broadcast([D, GROUP, D]), ALU.mult).then_inc(kv1_ready, 1)
            v.tensor_tensor(h[:, :, :], h[:, :, :], x1[:, :, :], ALU.add)
            done()
            for r in range(ROUNDS):
                dve.wait_ge(lin_text_done, r + 1)
                v.tensor_tensor(text_tiles(h, r), text_tiles(h, r),
                                bank[1 + r][:, :].rearrange("p (b d) -> p b d", d=D), ALU.add)
            dve.wait_ge(lin_patch_done, 1)
            v.tensor_tensor(h[:, 0:TILES:PER_ROUND, :], h[:, 0:TILES:PER_ROUND, :],
                            bank[7][:, 0:ROUNDS * D].rearrange("p (r d) -> p r d", d=D), ALU.add)
            done()
            normalise([(h[:, :, :], dev[:, :, :], sq[:, :, :], x2[:, :, :])], "rows", D, x2_ready)

            for s in range(SLOTS):
                v.memset(part[:, s, :], 0.0).then_inc(slot_free, 1)
            v.memset(y[:, :], 0.0).then_inc(y_free, 1)
            done()

            def search(tile, head):
                if head == 0:
                    wait_apart(dve, scores_copied, tile + 1, searches_begun)
                both = range(2)
                src = [scores[:, head, s, :] for s in both]
                for s in both:
                    v.max(half_top[:, s, 0:8], src[s])
                done()
                for s in both:
                    v.max_index(half_idx[:, s, 0:8], half_top[:, s, 0:8], src[s])
                    v.match_replace(rest[:, s, :], half_top[:, s, 0:8], src[s], DROPPED)
                done()
                for s in both:
                    v.max(half_top[:, s, 8:16], rest[:, s, :])
                done()
                for s in both:
                    last = v.max_index(half_idx[:, s, 8:16], half_top[:, s, 8:16], rest[:, s, :])
                if head == HEADS - 1:
                    last.then_inc(scores_used, 1)
                done()
                v.tensor_scalar(half_key[:, 0, :], half_idx[:, 0, :], float(head * NK * NK), None, ALU.add)
                v.tensor_scalar(half_key[:, 1, :], half_idx[:, 1, :], float(NK), None, ALU.mult)
                done()
                for dst, half in ((cand, half_top), (cand_row, half_key)):
                    at = 0
                    for a, n, cols in BLOCKS:
                        v.tensor_tensor(dst[:, at:at + n * cols].rearrange("p (a b) -> p a b", b=cols),
                                        half[:, 0, a:a + n].unsqueeze(2).to_broadcast([P, n, cols]),
                                        half[:, 1:2, 0:cols].to_broadcast([P, n, cols]), ALU.add)
                        at += n * cols
                done()
                v.max(best[:, head, 0:8], cand[:, :])
                done()
                v.max_index(best_at[:, 0:8], best[:, head, 0:8], cand[:, :])
                v.match_replace(cand_rest[:, :], best[:, head, 0:8], cand[:, :], DROPPED)
                done()
                v.max(best[:, head, 8:16], cand_rest[:, :])
                v.tensor_scalar(neg_best[:, head:head + 1], best[:, head, 0:1], -1.0, None, ALU.mult).then_inc(best_ready, 1)
                done()
                v.max_index(best_at[:, 8:16], best[:, head, 8:16], cand_rest[:, :])
                done()
                v.tensor_copy(best_place[:, :], best_at[:, :])
                done()
                v.tensor_tensor(picked[:, :, :], over(best_place[:, :], [P, TOP, CAND]),
                                place_f[:, :].unsqueeze(1).to_broadcast([P, TOP, CAND]), ALU.is_equal)
                done()
                v.tensor_tensor(picked_row[:, :, :], picked[:, :, :],
                                cand_row[:, :].unsqueeze(1).to_broadcast([P, TOP, CAND]), ALU.mult)
                done()
                v.tensor_reduce(best_row[:, :], picked_row[:, :, :], X, ALU.add)
                done()
                v.tensor_copy(rows[:, head, :], best_row[:, :]).then_inc(rows_ready, 1)

            def weighted_sum(tile, head, kv):
                slot = head % SLOTS
                dve.wait_ge(weight_ready, tile * HEADS + head + 1)
                v.reciprocal(weight_inv[:, head:head + 1], weight_sum[:, head:head + 1])
                done()
                v.tensor_scalar(weight_n[:, :], weight[:, head, :], weight_inv[:, head:head + 1], None, ALU.mult)
                done()
                dve.wait_ge(slot_filled[slot], (tile * (HEADS // SLOTS) + head // SLOTS + 1) * TOP * 16)
                for k in range(TOP):
                    a = k % 4
                    if k < 4:
                        v.tensor_scalar(part[:, a, :], gathered[:, slot, k, :], weight_n[:, k:k + 1], None, ALU.mult)
                    else:
                        last = v.scalar_tensor_tensor(part[:, a, :], gathered[:, slot, k, :], weight_n[:, k:k + 1],
                                                      part[:, a, :], ALU.mult, ALU.add)
                    if a == 3:
                        done()
                last.then_inc(slot_free, 1)
                v.tensor_tensor(half_sum[:, :, :], part[:, 0:2, :], part[:, 2:4, :], ALU.add)
                done()
                last = v.tensor_tensor(kv[:, :, head, :], half_sum[:, 0, :].rearrange("p (s d) -> p s d", d=D),
                                       half_sum[:, 1, :].rearrange("p (s d) -> p s d", d=D), ALU.add)
                if head == HEADS - 1:
                    last.then_inc(kv_ready, 1)

            for head in range(HEADS):
                search(0, head)

            def tile_step(tile, text, b):
                kv = kv_text if text else kv_patch
                for head in range(HEADS):
                    weighted_sum(tile, head, kv)
                    search(tile + 1, head)
                if text:
                    v.tensor_copy(text_mask[:, 0:P], batch_window[:, bass.ds((GROUP - 1) * PATCHES - b * PATCHES, P)])
                done()
                mask = text_mask if text else patch_mask
                width = 2 * P if text else P
                for i in range(HEADS):
                    if i >= 2:
                        dve.wait_ge(prob_ready, tile * HEADS + i - 1)
                    dve.wait_ge(sim_done, tile * HEADS + i + 1)
                    v.tensor_tensor(masked[:, i % 2, 0:width], sim[i % 2][:, 0:width], mask[:, 0:width], ALU.add)
                    done()
                    v.tensor_reduce(neg_max[:, i:i + 1], masked[:, i % 2, 0:width], X, ALU.max,
                                    negate=True).then_inc(sim_masked, 1)
                dve.wait_ge(av_done, (tile + 1) * HEADS)
                v.reciprocal(prob_inv[:, :], prob_sum[:, :])
                done()
                v.tensor_tensor(attended[:, :].rearrange("p (h d) -> p h d", d=D),
                                bank[6][:, :].rearrange("p (h d) -> p h d", d=D),
                                over(prob_inv[:, :], [P, HEADS, D]), ALU.mult).then_inc(av_scaled, 1)
                dve.wait_ge(y_done, tile + 1)
                dve.wait_ge(y_free, tile + 1)
                v.tensor_tensor(y[:, :], bank[7][:, 2 * P:2 * P + D], h[:, bass.ds(tile, 1), :].rearrange("p a d -> p (a d)"),
                                ALU.add).then_inc(y_ready, 1)

            with nc.Fori(0, ROUNDS, engines=[dve.engine]) as r:
                tile_step(r * PER_ROUND, False, None)
                with nc.Fori(0, GROUP, engines=[dve.engine]) as b:
                    tile_step(r * PER_ROUND + 1 + b, True, b)


def kernel(**inputs):
    import numpy as np
    import concourse.bacc as bacc
    from concourse import mybir as _mybir
    from concourse.bass_utils import run_bass_kernel_spmd as run

    a = {k: np.asarray(t) for k, t in inputs.items()}

    x = a["x"].reshape(BATCH, 3, 4, 16, 4, 16).transpose(1, 3, 5, 0, 2, 4).reshape(KPATCH, P, ROUNDS * P)
    tables = np.zeros((EMB, VCHUNKS * P), np.float32)
    for i, (name, at) in enumerate([("et", 0), ("fc", 64), ("sc", 128), ("of", 256), ("tt", 384), ("rc", 448)]):
        e = a["L0_txt_E_" + name]
        tables[16 * i:16 * (i + 1), at:at + e.shape[0]] = e.T
    arrays = {
        "patches": x.transpose(1, 0, 2),
        "tok_w": a["L0_tok_W"].T.reshape(KPATCH, P, D).transpose(1, 0, 2),
        "tok_b": a["L0_tok_b"].reshape(1, D),
        "tokens": np.stack([a[n].reshape(-1) for n in ("x_txt", "itok_BS_0_255", "itok_BS_0_511", "itok_BS_0_127",
                                                       "itok_BS_0_63", "itok_BS_0_3")]),
        "tables": tables.reshape(EMB, VCHUNKS, P),
        "txt_w": a["L0_txt_W"].T,
        "vectors": np.concatenate([a[n].reshape(-1) for n in (
            "L0_txt_b", "L0_txt_gamma", "L0_txt_beta", "L0_attn_kln_weight", "L0_attn_kln_bias",
            "L0_attn_vln_weight", "L0_attn_vln_bias")]).reshape(1, 7 * D),
        "pk_w": a["L0_ffn_Wq_pk"].reshape(D, 2, HEADS, KD).transpose(3, 2, 1, 0).reshape(KD, 2 * HEADS, D),
        "pk_keys": a["L0_ffn_pk_keys"].transpose(3, 2, 0, 1).reshape(KD, 2 * HEADS, NK),
        "q_w": a["L0_ffn_Wq"],
        "kv_table": np.concatenate([a["L0_ffn_keys_table"], a["L0_ffn_values_table"]], axis=1),
        "o_w": a["L0_ffn_Wo"].reshape(4, P, D).transpose(1, 0, 2),
    }
    arrays = {k: np.ascontiguousarray(t) for k, t in arrays.items()}
    nc = bacc.Bacc("TRN2", target_bir_lowering=False, num_devices=1)
    args = [nc.dram_tensor(k, t.shape, _mybir.dt.from_np(t.dtype), kind="ExternalInput").ap()
            for k, t in arrays.items()]
    args.append(nc.dram_tensor("out", (TILES * P, D), _mybir.dt.float32, kind="ExternalOutput").ap())
    build(nc, *args)
    tiles = run(nc, [arrays], core_ids=[0]).results[0]["out"].reshape(ROUNDS, PER_ROUND, P, D)
    patch = tiles[:, 0].reshape(BATCH, PATCHES, D)
    text = tiles[:, 1:].reshape(BATCH, P, D)
    return np.concatenate([patch, text], axis=1)
```

```python
import concourse.bass as bass
from concourse import mybir
from contextlib import ExitStack

F32 = mybir.dt.float32
BF16 = mybir.dt.bfloat16
I32 = mybir.dt.int32
U32 = mybir.dt.uint32
ALU = mybir.AluOpType
ACT = mybir.ActivationFunctionType
X = mybir.AxisListType.X

P = 128
D = 64
HEADS = 8
HC = D // HEADS
BATCH = 16
PATCHES = 16
SEQ = PATCHES + P
GROUP = P // PATCHES
ROUNDS = BATCH // GROUP
PER_ROUND = 1 + GROUP
TILES = ROUNDS * PER_ROUND
KPATCH = 3 * 16 * 16 // P
VCHUNKS = 4
EMB = 96
NK = 64
TOP = 16
KD = D // 2
SLOTS = 3
NEG = -3.0e38
DROPPED = -3.4028235e38
GATHERED = 6
DENSE = HEADS - GATHERED
CHUNKS = NK * NK // P
GROUPS = CHUNKS // 2
SEARCHED = [0, 1, 2, GATHERED, 3, 4, 5, GATHERED + 1]
BESIDE = {0: 6, 1: 5, 2: 5, GATHERED: 4, 3: 6, 4: 6}
MAGIC = 12582912.0

BATCH_RUNS = [[(0, 4), (4, GROUP)], [(0, GROUP - 1)]]
NEXT_FRONT = (0, 4)

BLOCKS = [(0, 1, 16), (1, 1, 8), (2, 2, 5), (4, 4, 3), (8, 8, 1)]
CAND = sum(rows * cols for _, rows, cols in BLOCKS)
PLACE = 2 * HEADS * NK * NK


def build(nc, patches, tok_w, tok_b, tokens, tables, txt_w, vectors, pk_w, pk_keys, q_w, kv_table, o_w, out):
    with ExitStack() as ctx:
        def sb(name, shape, dt=F32):
            return ctx.enter_context(nc.sbuf_tensor(name, shape, dt))

        def sem(name):
            return ctx.enter_context(nc.semaphore(name))

        patches_sb = sb("patches_sb", [P, KPATCH, ROUNDS * P])
        tok_w_sb = sb("tok_w_sb", [P, KPATCH, D])
        tok_b_sb = sb("tok_b_sb", [P, D])
        tokens_sb = sb("tokens_sb", [P, VCHUNKS, GROUP * P], I32)
        onehot = tokens_sb[:, :, :].bitcast(F32)
        tables_sb = sb("tables_sb", [EMB, VCHUNKS, P])
        txt_w_sb = sb("txt_w_sb", [EMB, D])
        w_eff = sb("w_eff", [EMB, D])
        w_stat = sb("w_stat", [EMB, 4])
        projected = sb("projected", [P, VCHUNKS, D])
        vec_sb = sb("vec_sb", [P, 7, D])
        pk_w_sb = sb("pk_w_sb", [KD, 2 * HEADS, D])
        pk_keys_sb = sb("pk_keys_sb", [KD, 2 * HEADS, NK])
        pk_fold = sb("pk_fold", [D, HEADS * 2 * NK])
        q_w_sb = sb("q_w_sb", [D, HEADS * D])
        o_w_sb = sb("o_w_sb", [P, 4, D])

        ones = sb("ones", [P, P])
        ident = sb("ident", [P, P])
        vocab_i = sb("vocab_i", [P, 2], I32)
        vocab_f = sb("vocab_f", [P, 2])
        place_i = sb("place_i", [P, CAND], I32)
        place_f = sb("place_f", [P, CAND])
        batch_of_row = sb("batch_of_row", [P, GROUP])
        head_blocks = sb("head_blocks", [D, D])
        patch_mask = sb("patch_mask", [P, P])
        text_mask = sb("text_mask", [P, P])
        batch_window = sb("batch_window", [P, 2 * P - PATCHES])
        eps = sb("eps", [P, 1])

        h = sb("h", [P, TILES, D])
        x1 = sb("x1", [P, PER_ROUND, D])
        dev = sb("dev", [P, PER_ROUND, D])
        sq = sb("sq", [P, PER_ROUND, D])
        x2 = sb("x2", [P, PER_ROUND, D])
        k1 = sb("k1", [P, PER_ROUND, D])
        v1 = sb("v1", [P, PER_ROUND, D])
        v1_split = sb("v1_split", [P, GROUP, D])
        mean = sb("mean", [P, PER_ROUND * HEADS])
        var = sb("var", [P, PER_ROUND * HEADS])
        std = sb("std", [P, PER_ROUND * HEADS])
        kv1 = sb("kv1", [D, GROUP, D])
        patch_out_t = sb("patch_out_t", [D, P])
        x1_t = sb("x1_t", [D, PER_ROUND * P])
        x2_t = sb("x2_t", [D, (TILES + 1) * P])

        x2_t_next = sb("x2_t_next", [D, P])
        scores = sb("scores", [P, HEADS, 2, NK])
        rest = sb("rest", [P, 2, NK])
        half_top = sb("half_top", [P, 2, TOP])
        half_idx = sb("half_idx", [P, 2, TOP], U32)
        half_key = sb("half_key", [P, 2, TOP])
        cand = sb("cand", [P, CAND])
        cand_row = sb("cand_row", [P, CAND])
        cand_rest = sb("cand_rest", [P, CAND])
        best_at = sb("best_at", [P, TOP], U32)
        best_place = sb("best_place", [P, TOP])
        picked = sb("picked", [P, TOP, CAND])
        best_row = sb("best_row", [P, TOP])
        best = sb("best", [P, HEADS, TOP])
        neg_best = sb("neg_best", [P, HEADS])
        rows = sb("rows", [P, HEADS, TOP], I32)
        weight = sb("weight", [P, HEADS, TOP])
        weight_sum = sb("weight_sum", [P, HEADS])
        weight_inv = sb("weight_inv", [P, HEADS])
        gathered = sb("gathered", [P, SLOTS, TOP, P])
        table_sb = sb("table_sb", [P, DENSE, CHUNKS, P])
        spread = sb("spread", [P, CHUNKS, 2, NK], BF16)
        ident_b = sb("ident_b", [P, P], BF16)
        key_b = sb("key_b", [P, NK], BF16)
        key_i = sb("key_i", [P, NK], I32)
        half_idx_f = sb("half_idx_f", [P, 2, TOP])
        chosen = sb("chosen", [P, CAND])
        row_count = sb("row_count", [P, TOP])
        hot = sb("hot", [P, TOP, P], BF16)
        reach_t = sb("reach_t", [P, DENSE, P], BF16)
        score_t = sb("score_t", [P, P])
        score_rest = sb("score_rest", [P, 2, P])
        score_parts = sb("score_parts", [P, DENSE, 3, P], BF16)
        grid_exp = sb("grid_exp", [P, 2, 2 * P])
        grid_w = sb("grid_w", [P, 2, 2 * P])
        kv_patch = sb("kv_patch", [P, 2, HEADS, D])
        kv_text = sb("kv_text", [P, 2, HEADS, D])
        q_t = sb("q_t", [P, 4, P])
        k_t_patch = sb("k_t_patch", [P, 4, P])
        k_t_text = sb("k_t_text", [P, 4, P])
        neg_max = sb("neg_max", [P, HEADS])
        prob = sb("prob", [P, 2, 2 * P])
        prob_sum = sb("prob_sum", [P, HEADS])
        prob_inv = sb("prob_inv", [P, HEADS])
        prob_t = sb("prob_t", [P, 2, 2 * P])
        attended = sb("attended", [P, HEADS * D])
        attended_t = sb("attended_t", [P, 4, P])
        y = sb("y", [P, D])

        bank = [ctx.enter_context(nc.psum_tensor(f"bank{i}", [P, 512], F32)) for i in range(8)]

        patch_loaded = sem("patch_loaded")
        txt_w_loaded = sem("txt_w_loaded")
        tokens_loaded = [sem(f"tokens_loaded{r}") for r in range(ROUNDS)]
        vec_loaded = sem("vec_loaded")
        pk_loaded = sem("pk_loaded")
        late_loaded = sem("late_loaded")
        consts_made = sem("consts_made")
        w_summed = sem("w_summed")
        w_total = sem("w_total")
        w_made = sem("w_made")
        fold_done = sem("fold_done")
        fold_copied = sem("fold_copied")
        tables_done = sem("tables_done")
        tables_copied = sem("tables_copied")
        onehot_made = sem("onehot_made")
        patch_embedded = sem("patch_embedded")
        text_embedded = sem("text_embedded")
        var_ready = sem("var_ready")
        std_ready = sem("std_ready")
        x1_ready = sem("x1_ready")
        x1_t_done = sem("x1_t_done")
        x1_t_copied = sem("x1_t_copied")
        kv1_in = sem("kv1_in")
        kv1_done = sem("kv1_done")
        kv1_ready = sem("kv1_ready")
        lin_text_done = sem("lin_text_done")
        lin_patch_t_done = sem("lin_patch_t_done")
        lin_patch_t_copied = sem("lin_patch_t_copied")
        lin_patch_done = sem("lin_patch_done")
        x2_ready = sem("x2_ready")
        x2_t_done = sem("x2_t_done")
        x2_t_copied = sem("x2_t_copied")

        x2_next_ready = sem("x2_next_ready")
        scores_done = sem("scores_done")
        scores_copied = sem("scores_copied")
        best_ready = sem("best_ready")
        weight_ready = sem("weight_ready")
        rows_ready = sem("rows_ready")
        searches_begun = sem("searches_begun")
        gathers_begun = sem("gathers_begun")
        slot_filled = [sem(f"slot_filled{s}") for s in range(SLOTS)]
        rows_weighted = sem("rows_weighted")
        rows_summed = sem("rows_summed")
        kv_copied = sem("kv_copied")
        q_done = sem("q_done")
        q_copied = sem("q_copied")
        k_t_done = sem("k_t_done")
        k_t_copied = sem("k_t_copied")
        sim_done = sem("sim_done")
        max_ready = sem("max_ready")
        prob_ready = sem("prob_ready")
        prob_t_done = sem("prob_t_done")
        prob_t_copied = sem("prob_t_copied")
        av_done = sem("av_done")
        av_scaled = sem("av_scaled")
        at_t_done = sem("at_t_done")
        at_t_copied = sem("at_t_copied")
        y_done = sem("y_done")
        table_loaded = sem("table_loaded")
        hot_ready = sem("hot_ready")
        turned_done = sem("turned_done")
        turned_copied = sem("turned_copied")
        parts_ready = sem("parts_ready")
        grid_scored = sem("grid_scored")
        grid_expd = sem("grid_expd")
        grid_masked = sem("grid_masked")
        grid_mixed = sem("grid_mixed")
        dense_done = sem("dense_done")
        dense_copied = sem("dense_copied")
        y_ready = sem("y_ready")
        y_stored = sem("y_stored")
        y_free = sem("y_free")

        sim = [bank[4], bank[0]]
        turned = [[bank[0], bank[4]], [bank[0], bank[4]], [bank[2], bank[7]], [bank[2], bank[7]]]
        grid = [bank[2], bank[7]]

        block = ctx.enter_context(nc.Block())

        VEC = {name: i for i, name in enumerate(["b", "gamma", "beta", "k_w", "k_b", "v_w", "v_b"])}

        def vec(name, n):
            return vec_sb[:, VEC[name]:VEC[name] + 1, :].to_broadcast([P, n, D])

        def over(stat, shape):
            return stat.unsqueeze(len(shape) - 1).to_broadcast(shape)

        QUADS = (PER_ROUND + 3) // 4

        def copy_transposed(act, dst, base, r, done, copied):
            for g in range(QUADS):
                n = min(4, PER_ROUND - 4 * g) * P
                at = (base + 4 * g) * P
                act.wait_ge(done, r * QUADS + g + 1)
                nc.scalar.copy(dst[:, at:at + n], bank[5 + g % 2][0:D, 0:n]).then_inc(copied, 1)

        MASKED, SCORED, at = {}, {}, 0
        for head in SEARCHED:
            end = at + BESIDE.get(head, 0)
            MASKED[head] = list(range(at, end))
            SCORED[head] = [g for g in range(at + 2, end + 2) if g < DENSE * GROUPS]
            at = end
        LAST_PAIR, DENSE_PAIR = GATHERED // 2 - 1, GATHERED // 2
        PAIR_ORDER = [0, 1, DENSE_PAIR, LAST_PAIR]

        def nth_head(head):
            return 2 * PAIR_ORDER.index(head // 2) + head % 2

        def wait_apart(eng, semaphore, value, passed):
            eng.wait_ge(semaphore, value)
            eng.sem_inc(passed, 1)

        @block.sync
        def _(sp):
            sp.dma_start(txt_w_sb[:, :], txt_w).then_inc(txt_w_loaded, 16)
            sp.dma_start(tables_sb[:, :, :], tables).then_inc(txt_w_loaded, 16)
            half = P // 2

            def load_tokens(r):
                cols = slice(r * GROUP * P, (r + 1) * GROUP * P)
                for kind, (low, high, chunk) in enumerate([(0, half, 0), (half, P, 0), (0, P, 1), (0, P, 2),
                                                           (0, half, 3), (half, P, 3)]):
                    sp.dma_start(tokens_sb[low:high, chunk, :],
                                 tokens[kind:kind + 1, cols].partition_broadcast(high - low)
                                 ).then_inc(tokens_loaded[r], 16)

            load_tokens(0)
            sp.dma_start(q_w_sb[:, :], q_w).then_inc(late_loaded, 16)
            sp.dma_start(o_w_sb[:, :, :], o_w).then_inc(late_loaded, 16)
            for i in range(DENSE):
                first = (GATHERED + i) * NK * NK
                sp.dma_start(table_sb[:, i, :, :], kv_table[first:first + NK * NK, :].rearrange("(c p) d -> p c d", p=P)
                             ).then_inc(table_loaded, 16)
            sp.wait_ge(text_embedded, 1)
            load_tokens(1)

            def store(tile, at):
                sp.wait_ge(y_ready, tile + 1)
                sp.dma_start(out[at, :], y[:, :]).then_inc(y_stored, 16)
                sp.wait_ge(y_stored, (tile + 1) * 16)
                sp.sem_inc(y_free, 1)

            with nc.Fori(0, ROUNDS, engines=[sp.engine]) as r:
                store(r * PER_ROUND, bass.ds(r * PER_ROUND * P, P))
                with nc.Fori(0, GROUP, engines=[sp.engine]) as b:
                    store(r * PER_ROUND + 1 + b, bass.ds((r * PER_ROUND + 1 + b) * P, P))
            sp.wait_ge(y_stored, 16 * TILES)

        @block.gpsimd
        def _(pool):
            nc.gpsimd.memset(ones[:, :], 1.0)
            nc.gpsimd.memset(ident[:, :], 0.0)
            nc.gpsimd.memset(eps[:, :], 1e-5)
            nc.gpsimd.memset(batch_of_row[:, :], 1.0)
            nc.gpsimd.memset(head_blocks[:, :], 1.0 / SEQ)
            nc.gpsimd.memset(patch_mask[:, :], 0.0)
            nc.gpsimd.memset(text_mask[:, :], 0.0)
            nc.gpsimd.memset(batch_window[:, :], NEG)
            nc.gpsimd.memset(x2_t[:, TILES * P:], 0.0)
            nc.gpsimd.iota(vocab_i[:, 0:1], pattern=[[0, 1]], base=0, channel_multiplier=1)
            nc.gpsimd.iota(vocab_i[:, 1:2], pattern=[[0, 1]], base=0, channel_multiplier=1)
            nc.gpsimd.memset(spread[:, :, :, :], 0.0)
            nc.gpsimd.iota(key_i[:, :], pattern=[[1, NK]], base=0, channel_multiplier=0)
            nc.gpsimd.iota(place_i[:, :], pattern=[[1, CAND]], base=0, channel_multiplier=0)
            pool.drain()
            nc.gpsimd.iota(vocab_i[P // 2:, 1:2], pattern=[[0, 1]], base=0, channel_multiplier=1)
            pool.drain()
            nc.gpsimd.memset(batch_window[:, P - PATCHES:P], 0.0)
            nc.gpsimd.affine_select(out=ident[:, :], in_=ident[:, :], compare_op=ALU.not_equal, fill=1.0,
                                    base=0, pattern=[[-1, P]], channel_multiplier=1)

            def keep_block(t, width, fill, per):
                n = t.shape[1] // per
                v = t.rearrange("p (n c) -> p n c", c=per)
                for base, sign in ((0, 1), (width - 1, -1)):
                    nc.gpsimd.affine_select(out=v, in_=v, compare_op=ALU.is_ge, fill=fill, base=base,
                                            pattern=[[-sign * width, n], [0, per]], channel_multiplier=sign)
                    pool.drain()

            keep_block(batch_of_row[:, :], PATCHES, 0.0, 1)
            keep_block(head_blocks[:, :], HC, 0.0, HC)
            keep_block(patch_mask[:, :], PATCHES, NEG, PATCHES)
            for t in (patch_mask[:, :], text_mask[:, :]):
                nc.gpsimd.affine_select(out=t, in_=t, compare_op=ALU.is_ge, fill=NEG,
                                        base=0, pattern=[[-1, P]], channel_multiplier=1)
            nc.gpsimd.tensor_copy(place_f[:, :], place_i[:, :])
            nc.gpsimd.tensor_copy(key_b[:, :], key_i[:, :])
            nc.gpsimd.tensor_copy(ident_b[:, :], ident[:, :])
            flat = spread[:, :, :, :].rearrange("p c j i -> p (c j) i")
            nc.gpsimd.affine_select(out=flat[0:NK], in_=flat[0:NK], compare_op=ALU.not_equal, fill=1.0, base=0,
                                    pattern=[[0, NK], [-1, NK]], channel_multiplier=1)
            pool.drain()
            nc.gpsimd.affine_select(out=flat[NK:P], in_=flat[NK:P], compare_op=ALU.not_equal, fill=1.0, base=0,
                                    pattern=[[-1, NK], [0, NK]], channel_multiplier=1)
            pool.drain()
            nc.gpsimd.tensor_copy(vocab_f[:, :], vocab_i[:, :]).then_inc(consts_made, 1)

            def gather(tile, head):
                slot = head % SLOTS
                if not (isinstance(tile, int) and head < SLOTS):
                    pool.wait_ge(rows_summed, tile * GATHERED + head + 1 - SLOTS)
                wait_apart(pool, rows_ready, tile * GATHERED + head + 1, gathers_begun)
                for k in range(TOP):
                    nc.gpsimd.indirect_dma_start(
                        gathered[:, slot, k, :], None, kv_table,
                        bass.IndirectOffsetOnAxis(rows[:, head, k:k + 1], 0)).then_inc(slot_filled[slot], 16)

            for head in range(GATHERED):
                gather(0, head)
            with nc.Fori(1, TILES, engines=[pool.engine]) as tile:
                for head in range(GATHERED):
                    gather(tile, head)

        @block.scalar
        def _(act):
            act.dma_start(patches_sb[:, :, :], patches).then_inc(patch_loaded, 16)
            act.dma_start(tok_w_sb[:, :, :], tok_w).then_inc(patch_loaded, 16)
            act.dma_start(tok_b_sb[:, :], tok_b.partition_broadcast(P)).then_inc(patch_loaded, 16)
            act.dma_start(vec_sb[:, :, :].rearrange("p a d -> p (a d)"),
                          vectors.partition_broadcast(P)).then_inc(vec_loaded, 16)
            act.dma_start(pk_w_sb[:, :, :], pk_w).then_inc(pk_loaded, 16)
            act.dma_start(pk_keys_sb[:, :, :], pk_keys).then_inc(pk_loaded, 16)

            act.wait_ge(tables_done, 1)
            nc.scalar.copy(projected[:, :, :].rearrange("p c d -> p (c d)"),
                           bank[2][:, 0:VCHUNKS * D]).then_inc(tables_copied, 1)
            for i in range(2):
                act.wait_ge(fold_done, i + 1)
                nc.scalar.copy(pk_fold[:, i * 512:(i + 1) * 512], bank[i][0:D, :]).then_inc(fold_copied, 1)

            act.wait_ge(consts_made, 1)
            def front(r):
                for i, (n, scale, bias) in enumerate([(GROUP, 1.0 / D, eps[:, :]), (PER_ROUND, 1.0 / D, eps[:, :]),
                                                      (PER_ROUND * HEADS, 1.0 / (HC - 1), 0.0),
                                                      (PER_ROUND, 1.0 / D, eps[:, :])]):
                    if i == 3:
                        copy_transposed(act, x1_t, 0, r, x1_t_done, x1_t_copied)
                        act.wait_ge(lin_patch_t_done, r + 1)
                        nc.scalar.copy(patch_out_t[:, :], bank[4][0:D, 0:P]).then_inc(lin_patch_t_copied, 1)
                    act.wait_ge(var_ready, 4 * r + i + 1)
                    nc.scalar.activation(std[:, 0:n], var[:, 0:n], ACT.Sqrt, scale=scale,
                                         bias=bias).then_inc(std_ready, 1)
                copy_transposed(act, x2_t, r * PER_ROUND, r, x2_t_done, x2_t_copied)

            def copy_tokens(tile):
                nc.scalar.copy(x2_t_next[:, :], x2_t[:, bass.ds(tile * P, P)]).then_inc(x2_next_ready, 1)

            def copy_scores(tile, half):
                flat = scores[:, :, :, :].rearrange("p h s k -> p (h s k)")
                act.wait_ge(scores_done, 2 * tile + half + 1)
                nc.scalar.copy(flat[:, half * 512:(half + 1) * 512],
                               bank[0 if half else 5][:, :]).then_inc(scores_copied, 1)

            def copy_queries(tile):
                act.wait_ge(q_done, tile + 1)
                nc.scalar.mul(q_t[:, :, :].rearrange("p a b -> p (a b)"), bank[1][:, :], D ** -0.5).then_inc(q_copied, 1)

            def weigh_rows(tile, head):
                slot = head % SLOTS
                act.wait_ge(slot_filled[slot], (tile * (GATHERED // SLOTS) + head // SLOTS + 1) * TOP * 16)
                for k in range(TOP):
                    nc.scalar.mul(gathered[:, slot, k, :], gathered[:, slot, k, :],
                                  weight[:, head, k:k + 1]).then_inc(rows_weighted, 1)

            def weigh(tile, head):
                act.wait_ge(best_ready, tile * HEADS + SEARCHED.index(head) + 1)
                nc.scalar.activation(weight[:, head, :], best[:, head, :], ACT.Exp, bias=neg_best[:, head:head + 1],
                                     accum_out=weight_sum[:, head:head + 1]).then_inc(weight_ready, 1)

            def copy_turned(tile, i):
                act.wait_ge(turned_done, tile * DENSE + i + 1)
                nc.scalar.copy(reach_t[:, i, :], bank[3][:, 0:P])
                nc.scalar.copy(score_t[:, :], bank[3][:, P:2 * P])
                nc.scalar.copy(score_parts[:, i, 0, :], bank[3][:, P:2 * P]).then_inc(turned_copied, 1)

            def grid_exps(tile, groups):
                for g in groups:
                    act.wait_ge(grid_scored, tile * DENSE * GROUPS + g + 1)
                    nc.scalar.activation(grid_exp[:, g % 2, :], grid[g % 2][:, 0:2 * P], ACT.Exp).then_inc(grid_expd, 1)

            front(0)
            act.wait_ge(x2_t_copied, QUADS)
            copy_tokens(0)
            copy_scores(0, 0)
            copy_scores(0, 1)
            copy_tokens(1)
            for head in SEARCHED:
                weigh(0, head)
                if head >= GATHERED:
                    copy_turned(0, head - GATHERED)
                if head == 3:
                    copy_scores(1, 0)
            copy_queries(0)
            grid_exps(0, [0, 1])
            weigh_rows(0, 0)

            def tile_step(tile, text, last=False):
                k_t = k_t_text if text else k_t_patch
                width = 2 * P if text else P

                def turn_keys(j):
                    act.wait_ge(k_t_done, tile * 4 + PAIR_ORDER.index(j) + 1)
                    nc.scalar.copy(k_t[:, j, :], bank[3][:, j * P:(j + 1) * P]).then_inc(k_t_copied, 1)

                def exp_pair(j):
                    for head in (2 * j, 2 * j + 1):
                        act.wait_ge(max_ready, tile * HEADS + nth_head(head) + 1)
                        nc.scalar.activation(prob[:, head % 2, 0:width], sim[head % 2][:, 0:width], ACT.Exp,
                                             bias=neg_max[:, head:head + 1],
                                             accum_out=prob_sum[:, head:head + 1]).then_inc(prob_ready, 1)

                def copy_pair(j):
                    for head in (2 * j, 2 * j + 1):
                        act.wait_ge(prob_t_done, tile * HEADS + nth_head(head) + 1)
                        nc.scalar.copy(prob_t[:, head % 2, 0:width],
                                       turned[j][head % 2][:, 0:width]).then_inc(prob_t_copied, 1)

                weigh_rows(tile, 1)
                grid_exps(tile, SCORED[0])
                if not last:
                    copy_scores(tile + 1, 1)
                weigh_rows(tile, 2)
                if not last:
                    weigh(tile + 1, 0)
                turn_keys(0)
                grid_exps(tile, SCORED[1])
                weigh_rows(tile, 3)
                if not last:
                    weigh(tile + 1, 1)
                exp_pair(0)
                grid_exps(tile, SCORED[2][:3])
                copy_pair(0)
                grid_exps(tile, SCORED[2][3:])
                grid_exps(tile, SCORED[GATHERED])
                weigh_rows(tile, 4)
                if not last:
                    weigh(tile + 1, 2)
                    weigh(tile + 1, GATHERED)
                    copy_turned(tile + 1, 0)
                turn_keys(1)
                grid_exps(tile, SCORED[3])
                weigh_rows(tile, 5)
                if not last:
                    weigh(tile + 1, 3)
                exp_pair(1)
                grid_exps(tile, SCORED[4][:2])
                copy_pair(1)
                grid_exps(tile, SCORED[4][2:])
                turn_keys(DENSE_PAIR)
                turn_keys(LAST_PAIR)
                exp_pair(DENSE_PAIR)
                copy_pair(DENSE_PAIR)
                if not last:
                    weigh(tile + 1, 4)
                    copy_tokens(tile + 2)
                    copy_scores(tile + 2, 0)
                    copy_queries(tile + 1)
                exp_pair(LAST_PAIR)
                copy_pair(LAST_PAIR)
                if not last:
                    grid_exps(tile + 1, [0, 1])
                    weigh(tile + 1, 5)
                act.wait_ge(at_t_done, tile + 1)
                nc.scalar.copy(attended_t[:, :, :].rearrange("p a b -> p (a b)"), bank[3][:, :]).then_inc(at_t_copied, 1)
                if not last:
                    weigh_rows(tile + 1, 0)
                    weigh(tile + 1, GATHERED + 1)
                    copy_turned(tile + 1, 1)

            for r in range(ROUNDS):
                tile_step(r * PER_ROUND, False)
                for lo, hi in BATCH_RUNS[r]:
                    with nc.Fori(lo, hi, engines=[act.engine]) as b:
                        tile_step(r * PER_ROUND + 1 + b, True)
                    if (r, hi) == NEXT_FRONT:
                        front(r + 1)
                        act.wait_ge(x2_t_copied, (r + 2) * QUADS)
            tile_step(TILES - 1, True, last=True)

        @block.tensor
        def _(pe):
            mm = nc.tensor.matmul
            pe.wait_ge(consts_made, 1)
            pe.wait_ge(w_summed, 1)
            mm(bank[7][0:EMB, 0:1], ones[0:EMB, 0:EMB], w_stat[:, 0:1], start=True, stop=True).then_inc(w_total, 1)
            pe.wait_ge(patch_loaded, 48)
            for r in range(ROUNDS):
                for c in range(KPATCH):
                    last = mm(bank[3][:, r * D:(r + 1) * D], patches_sb[:, c, r * P:(r + 1) * P],
                              tok_w_sb[:, c, :], start=(c == 0), stop=(c == KPATCH - 1))
            last.then_inc(patch_embedded, 1)
            pe.wait_ge(w_made, 1)
            for c in range(VCHUNKS):
                last = mm(bank[2][:, c * D:(c + 1) * D], tables_sb[:, c, :], w_eff[:, :], start=True, stop=True)
            last.then_inc(tables_done, 1)
            pe.wait_ge(tables_copied, 1)
            pe.wait_ge(pk_loaded, 32)
            for half in range(2):
                for i in range(HEADS):
                    u = half * HEADS + i
                    last = mm(bank[half][0:D, i * NK:(i + 1) * NK], pk_w_sb[:, u, :], pk_keys_sb[:, u, :],
                              start=True, stop=True)
                last.then_inc(fold_done, 1)

            def transpose_tiles(src, r, done, copied):
                for g in range(QUADS):
                    if g >= 2:
                        pe.wait_ge(copied, r * QUADS + g - 1)
                    for i in range(min(4, PER_ROUND - 4 * g)):
                        last = nc.tensor.transpose(bank[5 + g % 2][0:D, i * P:(i + 1) * P],
                                                   src[:, 4 * g + i, :], ident[:, :])
                    last.then_inc(done, 1)

            def front(r):
                pe.wait_ge(onehot_made, (r + 1) * VCHUNKS)
                for b in range(GROUP):
                    for c in range(VCHUNKS):
                        last = mm(bank[4][:, b * D:(b + 1) * D], onehot[:, c, b * P:(b + 1) * P],
                                  projected[:, c, :], start=(c == 0), stop=(c == VCHUNKS - 1))
                last.then_inc(text_embedded, 1)
                pe.wait_ge(x1_ready, r + 1)
                transpose_tiles(x1, r, x1_t_done, x1_t_copied)
                pe.wait_ge(kv1_in, r + 1)
                mm(bank[3][0:D, :], k1[:, 0, :], v1_split[:, :, :].rearrange("p b d -> p (b d)"),
                   start=True, stop=False, skip_group_check=True)
                for b in range(GROUP):
                    last = mm(bank[3][0:D, b * D:(b + 1) * D], k1[:, 1 + b, :], v1[:, 1 + b, :],
                              start=False, stop=(b == GROUP - 1), skip_group_check=True)
                last.then_inc(kv1_done, 1)
                pe.wait_ge(kv1_ready, r + 1)
                pe.wait_ge(x1_t_copied, (r + 1) * QUADS)
                for b in range(GROUP):
                    last = mm(bank[4][0:D, b * PATCHES:(b + 1) * PATCHES], kv1[:, b, :],
                              x1_t[:, b * PATCHES:(b + 1) * PATCHES], start=True, stop=True)
                last.then_inc(lin_patch_t_done, 1)
                for b in range(GROUP):
                    last = mm(bank[0][:, b * D:(b + 1) * D], x1_t[:, (1 + b) * P:(2 + b) * P], kv1[:, b, :],
                              start=True, stop=True)
                last.then_inc(lin_text_done, 1)
                pe.wait_ge(lin_patch_t_copied, r + 1)
                nc.tensor.transpose(bank[4][:, P:P + D], patch_out_t[:, :], ident[0:D, 0:D]).then_inc(lin_patch_done, 1)
                pe.wait_ge(x2_ready, r + 1)
                transpose_tiles(x2, r, x2_t_done, x2_t_copied)
                pe.wait_ge(x2_t_copied, (r + 1) * QUADS)

            def score(tile, half):
                if half == 0:
                    pe.wait_ge(x2_next_ready, tile + 1)
                nc.tensor.matmul(bank[0 if half else 5][:, :], x2_t_next[:, :], pk_fold[:, half * 512:(half + 1) * 512],
                                 start=True, stop=True).then_inc(scores_done, 1)

            pe.wait_ge(fold_copied, 2)
            front(0)
            def turn(tile, i):
                pe.wait_ge(hot_ready, tile * DENSE + i + 1)
                for a in range(TOP):
                    mm(bank[3][:, 0:P], hot[:, a, :], ident_b[:, :], start=(a == 0), stop=(a == TOP - 1))
                nc.tensor.transpose(bank[3][:, P:2 * P],
                                    scores[:, GATHERED + i, :, :].rearrange("p s k -> p (s k)"),
                                    ident[:, :]).then_inc(turned_done, 1)

            def sum_rows(tile, head):
                if head == 0:
                    pe.wait_ge(q_copied, tile + 1)
                else:
                    pe.wait_ge(kv_copied, tile * GATHERED + head)
                for k in range(TOP):
                    if k % 4 == 0:
                        pe.wait_ge(rows_weighted, (tile * GATHERED + head) * TOP + k + 4)
                    last = mm(bank[1][:, 0:P], ident[:, :], gathered[:, head % SLOTS, k, :],
                              start=(k == 0), stop=(k == TOP - 1))
                last.then_inc(rows_summed, 1)

            def queries(tile):
                if not isinstance(tile, int) or tile > 0:
                    pe.wait_ge(kv_copied, tile * GATHERED)
                for j in range(4):
                    end = mm(bank[1][:, j * P:(j + 1) * P], q_w_sb[:, j * P:(j + 1) * P],
                             x2_t[:, bass.ds(tile * P, P)], start=True, stop=True)
                end.then_inc(q_done, 1)

            def score_group(tile, g):
                i = g // GROUPS
                base = tile * DENSE * GROUPS
                if g >= 2:
                    pe.wait_ge(grid_masked, base + g - 1)
                for c in range(2):
                    pick = spread[:, 2 * (g % GROUPS) + c, :, :].rearrange("p j i -> p (j i)")
                    for part in range(3):
                        mm(grid[g % 2][:, c * P:(c + 1) * P], pick, score_parts[:, i, part, :],
                           start=(part == 0), stop=(part == 2))
                    end = mm(grid[g % 2][:, (2 + c) * P:(3 + c) * P], pick, reach_t[:, i, :], start=True, stop=True)
                end.then_inc(grid_scored, 1)

            def mix_group(tile, g):
                i = g // GROUPS
                pe.wait_ge(grid_masked, tile * DENSE * GROUPS + g + 1)
                if g == GROUPS:
                    pe.wait_ge(dense_copied, tile * DENSE + 1)
                for c in range(2):
                    at = g % GROUPS * 2 + c
                    end = mm(bank[5][:, 0:P], grid_w[:, g % 2, c * P:(c + 1) * P], table_sb[:, i, at, :],
                             start=(at == 0), stop=(at == CHUNKS - 1))
                end.then_inc(dense_done if g % GROUPS == GROUPS - 1 else grid_mixed, 1)

            def dense_groups(tile, groups):
                for g in groups:
                    if g % GROUPS == 0:
                        pe.wait_ge(parts_ready, tile * DENSE + g // GROUPS + 1)
                    score_group(tile, g)
                    if g >= 2:
                        mix_group(tile, g - 2)

            score(0, 0)
            score(0, 1)
            pe.wait_ge(scores_copied, 1)
            score(1, 0)
            turn(0, 0)
            pe.wait_ge(turned_copied, 1)
            turn(0, 1)
            pe.wait_ge(late_loaded, 32)
            queries(0)
            dense_groups(0, [0, 1])
            pe.wait_ge(q_copied, 1)
            sum_rows(0, 0)
            pe.wait_ge(table_loaded, 16 * DENSE)
            pe.wait_ge(turned_copied, DENSE)

            def tile_step(tile, text, b, last=False):
                kv, k_t = (kv_text, k_t_text) if text else (kv_patch, k_t_patch)
                keys = ([k_t_patch] if text else []) + [k_t]
                vals = ([kv_patch] if text else []) + [kv]
                masks = [batch_window[:, bass.ds((GROUP - 1) * PATCHES - b * PATCHES, P)],
                         text_mask[:, :]] if text else [patch_mask[:, :]]

                def turn_keys(j):
                    if 2 * j < GATHERED:
                        pe.wait_ge(kv_copied, tile * GATHERED + 2 * j + 2)
                    else:
                        pe.wait_ge(dense_copied, (tile + 1) * DENSE)
                    nc.tensor.transpose(bank[3][:, j * P:(j + 1) * P],
                                        kv[:, 0, 2 * j:2 * j + 2, :].rearrange("p a d -> p (a d)"),
                                        ident[:, :]).then_inc(k_t_done, 1)

                def compare(j):
                    pe.wait_ge(k_t_copied, tile * 4 + PAIR_ORDER.index(j) + 1)
                    for head in (2 * j, 2 * j + 1):
                        lo = (head % 2) * D
                        for n, (key, mask) in enumerate(zip(keys, masks)):
                            part = sim[head % 2][:, n * P:(n + 1) * P]
                            mm(part, q_t[lo:lo + D, j, :], key[lo:lo + D, j, :], start=True, stop=False)
                            end = mm(part, ident[:, :], mask, start=False, stop=True)
                        end.then_inc(sim_done, 1)

                def turn_pair(j):
                    pe.wait_ge(prob_ready, tile * HEADS + nth_head(2 * j + 1) + 1)
                    for head in (2 * j, 2 * j + 1):
                        for n in range(len(keys)):
                            end = nc.tensor.transpose(turned[j][head % 2][:, n * P:(n + 1) * P],
                                                      prob[:, head % 2, n * P:(n + 1) * P], ident[:, :])
                        end.then_inc(prob_t_done, 1)

                def mix_pair(j):
                    for head in (2 * j, 2 * j + 1):
                        pe.wait_ge(prob_t_copied, tile * HEADS + nth_head(head) + 1)
                        for n, val in enumerate(vals):
                            end = mm(bank[6][:, head * D:(head + 1) * D], prob_t[:, head % 2, n * P:(n + 1) * P],
                                     val[:, 1, head, :], start=(n == 0), stop=(n == len(vals) - 1))
                        end.then_inc(av_done, 1)

                sum_rows(tile, 1)
                dense_groups(tile, SCORED[0])
                if not last:
                    score(tile + 1, 1)
                sum_rows(tile, 2)
                turn_keys(0)
                dense_groups(tile, SCORED[1][:2])
                if not last:
                    pe.wait_ge(scores_copied, 2 * tile + 4)
                compare(0)
                dense_groups(tile, SCORED[1][2:])
                sum_rows(tile, 3)
                turn_pair(0)
                dense_groups(tile, SCORED[2][:3])
                mix_pair(0)
                dense_groups(tile, SCORED[2][3:])
                dense_groups(tile, SCORED[GATHERED])
                sum_rows(tile, 4)
                if not last:
                    turn(tile + 1, 0)
                    pe.wait_ge(turned_copied, (tile + 1) * DENSE + 1)
                turn_keys(1)
                dense_groups(tile, SCORED[3][:2])
                compare(1)
                dense_groups(tile, SCORED[3][2:])
                sum_rows(tile, 5)
                turn_pair(1)
                dense_groups(tile, SCORED[4][:2])
                mix_pair(1)
                dense_groups(tile, SCORED[4][2:])
                for g in (DENSE * GROUPS - 2, DENSE * GROUPS - 1):
                    mix_group(tile, g)
                turn_keys(DENSE_PAIR)
                compare(DENSE_PAIR)
                turn_keys(LAST_PAIR)
                turn_pair(DENSE_PAIR)
                compare(LAST_PAIR)
                mix_pair(DENSE_PAIR)
                if not last:
                    score(tile + 2, 0)
                    queries(tile + 1)
                turn_pair(LAST_PAIR)
                mix_pair(LAST_PAIR)
                if not last:
                    dense_groups(tile + 1, [0, 1])
                pe.wait_ge(av_scaled, tile + 1)
                for j in range(4):
                    end = nc.tensor.transpose(bank[3][:, j * P:(j + 1) * P], attended[:, j * P:(j + 1) * P], ident[:, :])
                end.then_inc(at_t_done, 1)
                pe.wait_ge(at_t_copied, tile + 1)
                for j in range(4):
                    end = mm(bank[4][:, 0:D], attended_t[:, j, :], o_w_sb[:, j, :], start=(j == 0), stop=(j == 3))
                end.then_inc(y_done, 1)
                if not last:
                    sum_rows(tile + 1, 0)
                    turn(tile + 1, 1)
                    pe.wait_ge(turned_copied, (tile + 2) * DENSE)

            for r in range(ROUNDS):
                tile_step(r * PER_ROUND, False, None)
                for lo, hi in BATCH_RUNS[r]:
                    with nc.Fori(lo, hi, engines=[pe.engine]) as b:
                        tile_step(r * PER_ROUND + 1 + b, True, b)
                    if (r, hi) == NEXT_FRONT:
                        front(r + 1)
            tile_step(TILES - 1, True, GROUP - 1, last=True)

        @block.vector
        def _(dve):
            v = nc.vector
            done = dve.drain

            dve.wait_ge(txt_w_loaded, 32)
            v.tensor_reduce(w_stat[:, 0:1], txt_w_sb[:, :], X, ALU.add, apply_absolute_value=True).then_inc(w_summed, 1)
            dve.wait_ge(consts_made, 1)

            def pick_columns(c):
                column = vocab_f[:, 1:2] if c in (0, 3) else vocab_f[:, 0:1]
                v.tensor_scalar(onehot[:, c, :], tokens_sb[:, c, :], column, None,
                                ALU.is_equal).then_inc(onehot_made, 1)

            dve.wait_ge(w_total, 1)
            v.tensor_scalar(w_stat[:, 1:2], bank[7][0:EMB, 0:1], 1.0 / (EMB * D), None, ALU.mult)
            done()
            v.tensor_scalar(w_stat[:, 2:3], w_stat[:, 1:2], 1e-8, None, ALU.add)
            done()
            v.reciprocal(w_stat[:, 3:4], w_stat[:, 2:3])
            done()
            v.tensor_scalar(w_eff[:, :], txt_w_sb[:, :], w_stat[:, 3:4], None, ALU.mult)
            done()
            v.tensor_scalar(w_eff[:, :], w_eff[:, :], 1.0, -1.0, ALU.min, ALU.max)
            done()
            v.tensor_scalar(w_eff[:, :], w_eff[:, :], MAGIC, None, ALU.add)
            done()
            v.tensor_scalar(w_eff[:, :], w_eff[:, :], MAGIC, None, ALU.subtract)
            done()
            v.scalar_tensor_tensor(w_eff[:, :], w_eff[:, :], w_stat[:, 1:2], txt_w_sb[:, :],
                                   ALU.mult, ALU.subtract)
            done()
            v.tensor_tensor(w_eff[:, :], w_eff[:, :], txt_w_sb[:, :], ALU.add).then_inc(w_made, 1)
            v.tensor_scalar(place_f[:, :], place_f[:, :], float(PLACE), None, ALU.mult)
            dve.wait_ge(tokens_loaded[0], 6 * 16)
            for c in range(VCHUNKS):
                pick_columns(c)
            dve.wait_ge(patch_loaded, 48)
            dve.wait_ge(patch_embedded, 1)
            v.tensor_tensor(h[:, 0:TILES:PER_ROUND, :], bank[3][:, 0:ROUNDS * D].rearrange("p (r d) -> p r d", d=D),
                            tok_b_sb[:, :].unsqueeze(1).to_broadcast([P, ROUNDS, D]), ALU.add)
            dve.wait_ge(vec_loaded, 16)

            n_std = [0]

            def normalise(parts, groups, width, signal=None):
                at = 0
                for src, cen, squ, _ in parts:
                    n = src.shape[1]
                    v.tensor_reduce(mean[:, at:at + n], src, X, ALU.add)
                    at += n
                done()
                v.tensor_scalar(mean[:, 0:at], mean[:, 0:at], 1.0 / width, None, ALU.mult)
                done()
                at = 0
                for src, cen, squ, _ in parts:
                    n = src.shape[1]
                    v.tensor_tensor(cen, src, over(mean[:, at:at + n], [P, n, width]), ALU.subtract)
                    at += n
                done()
                for src, cen, squ, _ in parts:
                    v.tensor_tensor(squ, cen, cen, ALU.mult)
                done()
                at = 0
                for src, cen, squ, _ in parts:
                    n = src.shape[1]
                    last = v.tensor_reduce(var[:, at:at + n], squ, X, ALU.add)
                    at += n
                last.then_inc(var_ready, 1)
                n_std[0] += 1
                dve.wait_ge(std_ready, n_std[0])
                if groups == "heads":
                    v.tensor_scalar(std[:, 0:at], std[:, 0:at], 1e-5, None, ALU.add)
                    done()
                v.reciprocal(std[:, 0:at], std[:, 0:at])
                done()
                at = 0
                for src, cen, squ, dst in parts:
                    n = src.shape[1]
                    last = v.tensor_tensor(dst, cen, over(std[:, at:at + n], [P, n, width]), ALU.mult)
                    at += n
                if signal is not None:
                    last.then_inc(signal, 1)
                done()

            def front(r):
                t = r * PER_ROUND

                def tiles(a):
                    return a[:, t:t + PER_ROUND, :] if a is h else a[:, :, :]

                def text_tiles(a):
                    return a[:, t + 1:t + PER_ROUND, :] if a is h else a[:, 1:PER_ROUND, :]

                dve.wait_ge(text_embedded, r + 1)
                v.tensor_tensor(text_tiles(h), bank[4][:, :].rearrange("p (b d) -> p b d", d=D),
                                vec("b", GROUP), ALU.add)
                done()
                normalise([tuple(text_tiles(a) for a in (h, dev, sq, h))], "rows", D)
                for name, op in (("gamma", ALU.mult), ("beta", ALU.add)):
                    v.tensor_tensor(text_tiles(h), text_tiles(h), vec(name, GROUP), op)
                    done()
                normalise([tuple(tiles(a) for a in (h, dev, sq, x1))], "rows", D, x1_ready)
                normalise([tuple(tiles(a).rearrange("p t (h c) -> p (t h) c", c=HC) for a in (x1, dev, sq, dev))],
                          "heads", HC)
                for a, w in ((k1, "k_w"), (v1, "v_w")):
                    v.tensor_tensor(tiles(a), tiles(dev), vec(w, PER_ROUND), ALU.mult)
                done()
                for a, w in ((k1, "k_b"), (v1, "v_b")):
                    v.tensor_tensor(tiles(a), tiles(a), vec(w, PER_ROUND), ALU.add)
                done()
                v.tensor_tensor(v1_split[:, :, :], v1[:, 0:1, :].to_broadcast([P, GROUP, D]),
                                over(batch_of_row[:, :], [P, GROUP, D]), ALU.mult).then_inc(kv1_in, 1)
                v.tensor_tensor(tiles(h), tiles(h), tiles(x1), ALU.add)
                dve.wait_ge(kv1_done, r + 1)
                v.tensor_tensor(kv1[:, :, :], bank[3][0:D, :].rearrange("p (b d) -> p b d", d=D),
                                head_blocks[:, :].unsqueeze(1).to_broadcast([D, GROUP, D]),
                                ALU.mult).then_inc(kv1_ready, 1)
                done()
                dve.wait_ge(lin_text_done, r + 1)
                v.tensor_tensor(text_tiles(h), text_tiles(h), bank[0][:, :].rearrange("p (b d) -> p b d", d=D), ALU.add)
                dve.wait_ge(lin_patch_done, r + 1)
                v.tensor_tensor(h[:, t, :], h[:, t, :], bank[4][:, P:P + D], ALU.add)
                done()
                normalise([tuple(tiles(a) for a in (h, dev, sq, x2))], "rows", D, x2_ready)

            v.memset(y[:, :], 0.0).then_inc(y_free, 1)
            done()

            def mask_group(tile, g):
                dve.wait_ge(grid_expd, tile * DENSE * GROUPS + g + 1)
                if g % GROUPS >= 2:
                    dve.wait_ge(grid_mixed, tile * DENSE * (GROUPS - 1) + g // GROUPS * (GROUPS - 1) + g % GROUPS - 1)
                v.scalar_tensor_tensor(grid_w[:, g % 2, :], grid[g % 2][:, 2 * P:4 * P], float(TOP),
                                       grid_exp[:, g % 2, :], ALU.is_gt, ALU.mult).then_inc(grid_masked, 1)

            def split_scores(tile, i):
                dve.wait_ge(turned_copied, tile * DENSE + i + 1)
                v.tensor_tensor(score_rest[:, 0, :], score_t[:, :], score_parts[:, i, 0, :], ALU.subtract)
                done()
                v.tensor_copy(score_parts[:, i, 1, :], score_rest[:, 0, :])
                done()
                v.tensor_tensor(score_rest[:, 1, :], score_rest[:, 0, :], score_parts[:, i, 1, :], ALU.subtract)
                done()
                v.tensor_copy(score_parts[:, i, 2, :], score_rest[:, 1, :]).then_inc(parts_ready, 1)

            def step(now, groups, n):
                done()
                if n < len(groups):
                    mask_group(now, groups[n])

            def best_keys(tile, head):
                if head == 0:
                    wait_apart(dve, scores_copied, 2 * tile + 1, searches_begun)
                if head == GATHERED:
                    wait_apart(dve, scores_copied, 2 * tile + 2, searches_begun)
                both = range(2)
                src = [scores[:, head, s, :] for s in both]
                for s in both:
                    v.max(half_top[:, s, 0:8], src[s])
                done()
                for s in both:
                    v.max_index(half_idx[:, s, 0:8], half_top[:, s, 0:8], src[s])
                    v.match_replace(rest[:, s, :], half_top[:, s, 0:8], src[s], DROPPED)
                done()
                for s in both:
                    v.max(half_top[:, s, 8:16], rest[:, s, :])
                done()
                for s in both:
                    v.max_index(half_idx[:, s, 8:16], half_top[:, s, 8:16], rest[:, s, :])
                done()
                if head >= GATHERED:
                    v.tensor_copy(half_idx_f[:, :, :], half_idx[:, :, :])
                else:
                    v.tensor_scalar(half_key[:, 0, :], half_idx[:, 0, :], float(head * NK * NK), None, ALU.add)
                    v.tensor_scalar(half_key[:, 1, :], half_idx[:, 1, :], float(NK), None, ALU.mult)
                    done()

            def best_pairs(tile, head, now, groups):
                dense = head >= GATHERED
                for dst, half in ((cand, half_top), (cand_row, half_key))[:1 if dense else 2]:
                    at = 0
                    for a, n, cols in BLOCKS:
                        v.tensor_tensor(dst[:, at:at + n * cols].rearrange("p (a b) -> p a b", b=cols),
                                        half[:, 0, a:a + n].unsqueeze(2).to_broadcast([P, n, cols]),
                                        half[:, 1:2, 0:cols].to_broadcast([P, n, cols]), ALU.add)
                        at += n * cols
                step(now, groups, 0)
                v.max(best[:, head, 0:8], cand[:, :])
                if not dense:
                    v.tensor_tensor(cand_row[:, :], cand_row[:, :], place_f[:, :], ALU.add)
                done()
                if not dense:
                    v.max_index(best_at[:, 0:8], best[:, head, 0:8], cand[:, :])
                v.match_replace(cand_rest[:, :], best[:, head, 0:8], cand[:, :], DROPPED)
                step(now, groups, 1)
                v.max(best[:, head, 8:16], cand_rest[:, :])
                v.tensor_scalar(neg_best[:, head:head + 1], best[:, head, 0:1], -1.0, None, ALU.mult).then_inc(best_ready, 1)
                done()

            def find_rows(tile, head, now, groups):
                v.max_index(best_at[:, 8:16], best[:, head, 8:16], cand_rest[:, :])
                done()
                v.tensor_scalar(best_place[:, :], best_at[:, :], float(PLACE), None, ALU.mult)
                step(now, groups, 0)
                v.tensor_tensor(picked[:, :, :], cand_row[:, :].unsqueeze(1).to_broadcast([P, TOP, CAND]),
                                over(best_place[:, :], [P, TOP, CAND]), ALU.subtract)
                step(now, groups, 1)
                if len(groups) > 4:
                    mask_group(now, groups[4])
                v.tensor_reduce(best_row[:, :], picked[:, :, :], X, ALU.min, apply_absolute_value=True)
                step(now, groups, 2)
                step(now, groups, 3)
                v.tensor_copy(rows[:, head, :], best_row[:, :]).then_inc(rows_ready, 1)

            def mark_pairs(tile, head, now, groups):
                v.match_replace(chosen[:, :], best[:, head, 8:16], cand_rest[:, :], DROPPED)
                v.tensor_scalar(scores[:, head, 0, :], scores[:, head, 0, :], neg_best[:, head:head + 1], None, ALU.add)
                done()
                v.tensor_tensor(chosen[:, :], chosen[:, :], cand[:, :], ALU.not_equal)
                done()
                at = 0
                for a, n, cols in BLOCKS:
                    v.tensor_reduce(row_count[:, a:a + n],
                                    chosen[:, at:at + n * cols].rearrange("p (a b) -> p a b", b=cols), X, ALU.add)
                    at += n * cols
                done()
                for a in range(TOP):
                    v.tensor_scalar(hot[:, a, 0:NK], key_b[:, :], half_idx_f[:, 0, a:a + 1],
                                    row_count[:, a:a + 1], ALU.is_equal, ALU.mult)
                    end = v.tensor_scalar(hot[:, a, NK:P], key_b[:, :], half_idx_f[:, 1, a:a + 1],
                                          float(TOP - a), ALU.is_equal, ALU.mult)
                    if a % 4 == 2 and a // 4 < len(groups):
                        mask_group(now, groups[a // 4])
                end.then_inc(hot_ready, 1)

            def search(tile, head, now=None, groups=()):
                best_keys(tile, head)
                best_pairs(tile, head, now, groups[:2])
                if head < GATHERED:
                    find_rows(tile, head, now, groups[2:])
                else:
                    mark_pairs(tile, head, now, groups[2:])

            def take_rows(tile, head, kv):
                dve.wait_ge(rows_summed, tile * GATHERED + head + 1)
                v.reciprocal(weight_inv[:, head:head + 1], weight_sum[:, head:head + 1])
                done()
                v.tensor_scalar(kv[:, :, head, :], bank[1][:, 0:P].rearrange("p (s d) -> p s d", d=D),
                                weight_inv[:, head:head + 1], None, ALU.mult).then_inc(kv_copied, 1)

            def take_dense(tile, i, kv):
                head = GATHERED + i
                dve.wait_ge(dense_done, tile * DENSE + i + 1)
                v.reciprocal(weight_inv[:, head:head + 1], weight_sum[:, head:head + 1])
                done()
                v.tensor_scalar(kv[:, :, head, :], bank[5][:, 0:P].rearrange("p (s d) -> p s d", d=D),
                                weight_inv[:, head:head + 1], None, ALU.mult).then_inc(dense_copied, 1)

            front(0)
            for head in SEARCHED:
                if head == GATHERED + 1:
                    split_scores(0, 0)
                search(0, head)

            def next_front(r):
                dve.wait_ge(tokens_loaded[r], 6 * 16)
                for c in range(VCHUNKS):
                    pick_columns(c)
                front(r)

            def tile_step(tile, text, b, last=False):
                kv = kv_text if text else kv_patch
                width = 2 * P if text else P

                def attend(j):
                    for head in (2 * j, 2 * j + 1):
                        dve.wait_ge(sim_done, tile * HEADS + nth_head(head) + 1)
                        v.tensor_reduce(neg_max[:, head:head + 1], sim[head % 2][:, 0:width], X, ALU.max,
                                        negate=True).then_inc(max_ready, 1)

                def search_next(head):
                    if last:
                        for g in MASKED[head]:
                            mask_group(tile, g)
                    else:
                        search(tile + 1, head, tile, MASKED[head])

                take_rows(tile, 0, kv)
                search_next(0)
                split_scores(tile, 1)
                take_rows(tile, 1, kv)
                search_next(1)
                take_rows(tile, 2, kv)
                attend(0)
                search_next(2)
                take_dense(tile, 0, kv)
                search_next(GATHERED)
                take_rows(tile, 3, kv)
                search_next(3)
                if not last:
                    split_scores(tile + 1, 0)
                take_rows(tile, 4, kv)
                attend(1)
                search_next(4)
                take_dense(tile, 1, kv)
                take_rows(tile, 5, kv)
                if not last:
                    best_keys(tile + 1, 5)
                attend(DENSE_PAIR)
                if not last:
                    best_pairs(tile + 1, 5, tile, [])
                attend(LAST_PAIR)
                if not last:
                    find_rows(tile + 1, 5, tile, [])
                    best_keys(tile + 1, GATHERED + 1)
                dve.wait_ge(av_done, (tile + 1) * HEADS)
                v.reciprocal(prob_inv[:, :], prob_sum[:, :])
                done()
                v.tensor_tensor(attended[:, :].rearrange("p (h d) -> p h d", d=D),
                                bank[6][:, :].rearrange("p (h d) -> p h d", d=D),
                                over(prob_inv[:, :], [P, HEADS, D]), ALU.mult).then_inc(av_scaled, 1)
                if not last:
                    best_pairs(tile + 1, GATHERED + 1, tile, [])
                    mark_pairs(tile + 1, GATHERED + 1, tile, [])
                dve.wait_ge(y_done, tile + 1)
                dve.wait_ge(y_free, tile + 1)
                v.tensor_tensor(y[:, :], bank[4][:, 0:D], h[:, bass.ds(tile, 1), :].rearrange("p a d -> p (a d)"),
                                ALU.add).then_inc(y_ready, 1)
            for r in range(ROUNDS):
                tile_step(r * PER_ROUND, False, None)
                for lo, hi in BATCH_RUNS[r]:
                    with nc.Fori(lo, hi, engines=[dve.engine]) as b:
                        tile_step(r * PER_ROUND + 1 + b, True, b)
                    if (r, hi) == NEXT_FRONT:
                        next_front(r + 1)
            tile_step(TILES - 1, True, GROUP - 1, last=True)


def kernel(**inputs):
    import numpy as np
    import concourse.bacc as bacc
    from concourse import mybir as _mybir
    from concourse.bass_utils import run_bass_kernel_spmd as run

    a = {k: np.asarray(t) for k, t in inputs.items()}

    x = a["x"].reshape(BATCH, 3, 4, 16, 4, 16).transpose(1, 3, 5, 0, 2, 4).reshape(KPATCH, P, ROUNDS * P)
    tables = np.zeros((EMB, VCHUNKS * P), np.float32)
    for i, (name, at) in enumerate([("et", 0), ("fc", 64), ("sc", 128), ("of", 256), ("tt", 384), ("rc", 448)]):
        e = a["L0_txt_E_" + name]
        tables[16 * i:16 * (i + 1), at:at + e.shape[0]] = e.T
    arrays = {
        "patches": x.transpose(1, 0, 2),
        "tok_w": a["L0_tok_W"].T.reshape(KPATCH, P, D).transpose(1, 0, 2),
        "tok_b": a["L0_tok_b"].reshape(1, D),
        "tokens": np.stack([a[n].reshape(-1) for n in ("x_txt", "itok_BS_0_255", "itok_BS_0_511", "itok_BS_0_127",
                                                       "itok_BS_0_63", "itok_BS_0_3")]),
        "tables": tables.reshape(EMB, VCHUNKS, P),
        "txt_w": a["L0_txt_W"].T,
        "vectors": np.concatenate([a[n].reshape(-1) for n in (
            "L0_txt_b", "L0_txt_gamma", "L0_txt_beta", "L0_attn_kln_weight", "L0_attn_kln_bias",
            "L0_attn_vln_weight", "L0_attn_vln_bias")]).reshape(1, 7 * D),
        "pk_w": a["L0_ffn_Wq_pk"].reshape(D, 2, HEADS, KD).transpose(3, 2, 1, 0).reshape(KD, 2 * HEADS, D),
        "pk_keys": a["L0_ffn_pk_keys"].transpose(3, 2, 0, 1).reshape(KD, 2 * HEADS, NK),
        "q_w": a["L0_ffn_Wq"],
        "kv_table": np.concatenate([a["L0_ffn_keys_table"], a["L0_ffn_values_table"]], axis=1),
        "o_w": a["L0_ffn_Wo"].reshape(4, P, D).transpose(1, 0, 2),
    }
    arrays = {k: np.ascontiguousarray(t) for k, t in arrays.items()}
    nc = bacc.Bacc("TRN2", target_bir_lowering=False, num_devices=1)
    args = [nc.dram_tensor(k, t.shape, _mybir.dt.from_np(t.dtype), kind="ExternalInput").ap()
            for k, t in arrays.items()]
    args.append(nc.dram_tensor("out", (TILES * P, D), _mybir.dt.float32, kind="ExternalOutput").ap())
    build(nc, *args)
    tiles = run(nc, [arrays], core_ids=[0]).results[0]["out"].reshape(ROUNDS, PER_ROUND, P, D)
    patch = tiles[:, 0].reshape(BATCH, PATCHES, D)
    text = tiles[:, 1:].reshape(BATCH, P, D)
    return np.concatenate([patch, text], axis=1)
```

```python
import concourse.bass as bass
from concourse import mybir
from contextlib import ExitStack

F32 = mybir.dt.float32
BF16 = mybir.dt.bfloat16
I32 = mybir.dt.int32
U32 = mybir.dt.uint32
ALU = mybir.AluOpType
ACT = mybir.ActivationFunctionType
X = mybir.AxisListType.X

P = 128
D = 64
HEADS = 8
HC = D // HEADS
BATCH = 16
PATCHES = 16
SEQ = PATCHES + P
GROUP = P // PATCHES
ROUNDS = BATCH // GROUP
PER_ROUND = 1 + GROUP
TILES = ROUNDS * PER_ROUND
KPATCH = 3 * 16 * 16 // P
VCHUNKS = 4
EMB = 96
NK = 64
TOP = 16
KD = D // 2
SLOTS = 6
NEG = -3.0e38
DROPPED = -3.4028235e38
GATHERED = 6
DENSE = HEADS - GATHERED
CHUNKS = NK * NK // P
GROUPS = CHUNKS // 2
SEARCHED = [0, 1, 2, GATHERED, 3, 4, 5, GATHERED + 1]
BESIDE = {0: 6, 1: 5, 2: 5, GATHERED: 4, 3: 6, 4: 6}
MAGIC = 12582912.0

BATCH_RUNS = [[(0, 4), (4, GROUP)], [(0, GROUP - 1)]]
NEXT_FRONT = (0, 4)

BLOCKS = [(0, 1, 16), (1, 1, 8), (2, 2, 5), (4, 4, 3), (8, 8, 1)]
CAND = sum(rows * cols for _, rows, cols in BLOCKS)
PLACE = 2 * HEADS * NK * NK


def build(nc, patches, tok_w, tok_b, tokens, tables, txt_w, vectors, pk_w, pk_keys, q_w, kv_table, o_w, out):
    with ExitStack() as ctx:
        def sb(name, shape, dt=F32):
            return ctx.enter_context(nc.sbuf_tensor(name, shape, dt))

        def sem(name):
            return ctx.enter_context(nc.semaphore(name))

        gathered = sb("gathered", [P, SLOTS, TOP, P])
        last_slots = [gathered[:, SLOTS - 2 + i, :, :].rearrange("p k c -> p (k c)") for i in range(2)]
        third_last = gathered[:, SLOTS - 3, :, :].rearrange("p k c -> p (k c)")
        width = VCHUNKS * D
        projected = third_last[:, 0:width]
        projected_rest = third_last[:, width:3 * width].rearrange("p (a n) -> p a n", a=2)
        tables_sb = third_last[0:EMB, 3 * width:3 * width + VCHUNKS * P].rearrange("p (c n) -> p c n", c=VCHUNKS)
        width = KPATCH * ROUNDS * P
        patches_sb = last_slots[0][:, 0:width].rearrange("p (c n) -> p c n", c=KPATCH)
        tok_w_sb = last_slots[0][:, width:width + KPATCH * D].rearrange("p (c d) -> p c d", c=KPATCH)
        width = 2 * HEADS * D
        pk_w_sb = last_slots[1][0:KD, 0:width].rearrange("p (u d) -> p u d", d=D)
        pk_keys_sb = last_slots[1][0:KD, width:width + 2 * HEADS * NK].rearrange("p (u k) -> p u k", k=NK)
        tok_b_sb = sb("tok_b_sb", [P, D])
        tokens_sb = sb("tokens_sb", [P, VCHUNKS, GROUP * P], I32)
        txt_w_sb = sb("txt_w_sb", [EMB, D])
        w_eff = sb("w_eff", [EMB, D])
        w_stat = sb("w_stat", [EMB, 4])
        projected_parts = sb("projected_parts", [P, 3, VCHUNKS * D], BF16)
        vec_sb = sb("vec_sb", [P, 7, D])
        pk_fold = sb("pk_fold", [D, HEADS * 2 * NK])
        q_w_sb = sb("q_w_sb", [D, HEADS * D])
        o_w_sb = sb("o_w_sb", [P, 4, D])

        ones = sb("ones", [P, P])
        ident = sb("ident", [P, P])
        vocab_i = sb("vocab_i", [P, 2], I32)
        vocab_f = sb("vocab_f", [P, 2])
        place_i = sb("place_i", [P, CAND], I32)
        place_f = sb("place_f", [P, CAND])
        batch_of_row = sb("batch_of_row", [P, GROUP])
        head_blocks = sb("head_blocks", [D, D])
        patch_mask = sb("patch_mask", [P, P])
        text_mask = sb("text_mask", [P, P])
        batch_window = sb("batch_window", [P, 2 * P - PATCHES])
        eps = sb("eps", [P, 1])

        h = sb("h", [P, TILES, D])
        x1 = sb("x1", [P, PER_ROUND, D])
        x2 = sb("x2", [P, PER_ROUND, D])
        front_sb = sb("front_sb", [P, 4, PER_ROUND * D])
        dev, sq, k1, v1 = [front_sb[:, i, :].rearrange("p (t d) -> p t d", d=D) for i in range(4)]
        onehot = front_sb[:, :, :].rearrange("p a n -> p (a n)")[:, 0:VCHUNKS * GROUP * P // 2].bitcast(BF16)
        onehot = onehot.rearrange("p (c n) -> p c n", c=VCHUNKS)
        v1_split = sb("v1_split", [P, GROUP, D])
        mean = sb("mean", [P, PER_ROUND * HEADS])
        var = sb("var", [P, PER_ROUND * HEADS])
        std = sb("std", [P, PER_ROUND * HEADS])
        kv1 = sb("kv1", [D, GROUP, D])
        patch_out_t = sb("patch_out_t", [D, P])
        x1_t = sb("x1_t", [D, PER_ROUND * P])
        x2_t = sb("x2_t", [D, (TILES + 1) * P])

        x2_t_next = sb("x2_t_next", [D, P])
        scores = sb("scores", [P, HEADS, 2, NK])
        rest = sb("rest", [P, 2, NK])
        half_top = sb("half_top", [P, 2, TOP])
        half_idx = sb("half_idx", [P, 2, TOP], U32)
        half_key = sb("half_key", [P, 2, TOP])
        cand = sb("cand", [P, CAND])
        cand_row = sb("cand_row", [P, CAND])
        cand_rest = sb("cand_rest", [P, CAND])
        best_at = sb("best_at", [P, TOP], U32)
        best_place = sb("best_place", [P, TOP])
        picked = sb("picked", [P, TOP, CAND])
        best_row = sb("best_row", [P, TOP])
        best = sb("best", [P, HEADS, TOP])
        neg_best = sb("neg_best", [P, HEADS])
        rows = sb("rows", [P, HEADS, TOP], I32)
        weight = sb("weight", [P, HEADS, TOP])
        weight_sum = sb("weight_sum", [P, HEADS])
        weight_inv = sb("weight_inv", [P, HEADS])
        table_sb = sb("table_sb", [P, DENSE, CHUNKS, P])
        spread = sb("spread", [P, CHUNKS, 2, NK], BF16)
        ident_b = sb("ident_b", [P, P], BF16)
        ident_ranks = sb("ident_ranks", [P, TOP, P], BF16)
        key_b = sb("key_b", [P, NK], BF16)
        key_i = sb("key_i", [P, NK], I32)
        half_idx_f = sb("half_idx_f", [P, 2, TOP])
        chosen = sb("chosen", [P, CAND])
        row_count = sb("row_count", [P, TOP])
        hot = sb("hot", [P, TOP, P], BF16)
        reach_t = sb("reach_t", [P, DENSE, P], BF16)
        score_t = sb("score_t", [P, P])
        score_rest = sb("score_rest", [P, 2, P])
        score_parts = sb("score_parts", [P, DENSE, 3, P], BF16)
        grid_exp = sb("grid_exp", [P, 2, 2 * P])
        grid_w = sb("grid_w", [P, 2, 2 * P])
        kv_patch = sb("kv_patch", [P, 2, HEADS, D])
        kv_text = sb("kv_text", [P, 2, HEADS, D])
        q_t = sb("q_t", [P, 4, P])
        k_t_patch = sb("k_t_patch", [P, 4, P])
        k_t_text = sb("k_t_text", [P, 4, P])
        neg_max = sb("neg_max", [P, HEADS])
        prob = sb("prob", [P, 2, 2 * P])
        prob_sum = sb("prob_sum", [P, HEADS])
        prob_inv = sb("prob_inv", [P, HEADS])
        prob_t = sb("prob_t", [P, 2, 2 * P])
        attended = sb("attended", [P, HEADS * D])
        attended_t = sb("attended_t", [P, 4, P])
        y = sb("y", [P, D])

        bank = [ctx.enter_context(nc.psum_tensor(f"bank{i}", [P, 512], F32)) for i in range(8)]

        patch_loaded = sem("patch_loaded")
        txt_w_loaded = sem("txt_w_loaded")
        tokens_loaded = [sem(f"tokens_loaded{r}") for r in range(ROUNDS)]
        vec_loaded = sem("vec_loaded")
        pk_loaded = sem("pk_loaded")
        late_loaded = sem("late_loaded")
        first_consts_made = sem("first_consts_made")
        consts_made = sem("consts_made")
        ranks_made = sem("ranks_made")
        w_summed = sem("w_summed")
        w_total = sem("w_total")
        w_made = sem("w_made")
        fold_done = sem("fold_done")
        fold_copied = sem("fold_copied")
        tables_done = sem("tables_done")
        tables_copied = sem("tables_copied")
        projected_split = sem("projected_split")
        onehot_made = sem("onehot_made")
        patch_embedded = sem("patch_embedded")
        text_embedded = sem("text_embedded")
        var_ready = sem("var_ready")
        std_ready = sem("std_ready")
        x1_ready = sem("x1_ready")
        x1_t_done = sem("x1_t_done")
        x1_t_copied = sem("x1_t_copied")
        kv1_in = sem("kv1_in")
        kv1_done = sem("kv1_done")
        kv1_ready = sem("kv1_ready")
        lin_text_done = sem("lin_text_done")
        lin_patch_t_done = sem("lin_patch_t_done")
        lin_patch_t_copied = sem("lin_patch_t_copied")
        lin_patch_done = sem("lin_patch_done")
        x2_ready = sem("x2_ready")
        x2_t_done = sem("x2_t_done")
        x2_t_copied = sem("x2_t_copied")

        x2_next_ready = sem("x2_next_ready")
        scores_done = sem("scores_done")
        scores_copied = sem("scores_copied")
        best_ready = sem("best_ready")
        weight_ready = sem("weight_ready")
        rows_ready = sem("rows_ready")
        searches_begun = sem("searches_begun")
        gathers_begun = sem("gathers_begun")
        slot_filled = [sem(f"slot_filled{s}") for s in range(SLOTS)]
        rows_weighted = sem("rows_weighted")
        rows_summed = sem("rows_summed")
        kv_copied = sem("kv_copied")
        q_done = sem("q_done")
        q_copied = sem("q_copied")
        k_t_done = sem("k_t_done")
        k_t_copied = sem("k_t_copied")
        sim_done = sem("sim_done")
        max_ready = sem("max_ready")
        prob_ready = sem("prob_ready")
        prob_t_done = sem("prob_t_done")
        prob_t_copied = sem("prob_t_copied")
        av_done = sem("av_done")
        av_scaled = sem("av_scaled")
        at_t_done = sem("at_t_done")
        at_t_copied = sem("at_t_copied")
        y_done = sem("y_done")
        table_loaded = sem("table_loaded")
        hot_marked = sem("hot_marked")
        hot_ready = sem("hot_ready")
        turned_done = sem("turned_done")
        turned_copied = sem("turned_copied")
        parts_ready = sem("parts_ready")
        grid_scored = sem("grid_scored")
        grid_expd = sem("grid_expd")
        grid_masked = sem("grid_masked")
        grid_mixed = sem("grid_mixed")
        dense_done = sem("dense_done")
        dense_copied = sem("dense_copied")
        y_ready = sem("y_ready")
        y_stored = sem("y_stored")
        y_free = sem("y_free")

        sim = [bank[4], bank[0]]
        turned = [[bank[0], bank[4]], [bank[0], bank[4]], [bank[2], bank[7]], [bank[2], bank[7]]]
        grid = [bank[2], bank[7]]

        block = ctx.enter_context(nc.Block())

        VEC = {name: i for i, name in enumerate(["b", "gamma", "beta", "k_w", "k_b", "v_w", "v_b"])}

        def vec(name, n):
            return vec_sb[:, VEC[name]:VEC[name] + 1, :].to_broadcast([P, n, D])

        def over(stat, shape):
            return stat.unsqueeze(len(shape) - 1).to_broadcast(shape)

        QUADS = (PER_ROUND + 3) // 4

        def copy_transposed(act, dst, base, r, done, copied):
            for g in range(QUADS):
                n = min(4, PER_ROUND - 4 * g) * P
                at = (base + 4 * g) * P
                act.wait_ge(done, r * QUADS + g + 1)
                nc.scalar.copy(dst[:, at:at + n], bank[5 + g % 2][0:D, 0:n]).then_inc(copied, 1)

        MASKED, SCORED, at = {}, {}, 0
        for head in SEARCHED:
            end = at + BESIDE.get(head, 0)
            MASKED[head] = list(range(at, end))
            SCORED[head] = [g for g in range(at + 2, end + 2) if g < DENSE * GROUPS]
            at = end
        LAST_PAIR, DENSE_PAIR = GATHERED // 2 - 1, GATHERED // 2
        PAIR_ORDER = [0, 1, DENSE_PAIR, LAST_PAIR]

        def nth_head(head):
            return 2 * PAIR_ORDER.index(head // 2) + head % 2

        def wait_apart(eng, semaphore, value, passed):
            eng.wait_ge(semaphore, value)
            eng.sem_inc(passed, 1)

        @block.sync
        def _(sp):
            sp.dma_start(txt_w_sb[:, :], txt_w).then_inc(txt_w_loaded, 16)
            sp.dma_start(tables_sb[:, :, :], tables).then_inc(txt_w_loaded, 16)
            half = P // 2

            def load_tokens(r):
                cols = slice(r * GROUP * P, (r + 1) * GROUP * P)
                for kind, (low, high, chunk) in enumerate([(0, half, 0), (half, P, 0), (0, P, 1), (0, P, 2),
                                                           (0, half, 3), (half, P, 3)]):
                    sp.dma_start(tokens_sb[low:high, chunk, :],
                                 tokens[kind:kind + 1, cols].partition_broadcast(high - low)
                                 ).then_inc(tokens_loaded[r], 16)

            load_tokens(0)
            sp.dma_start(q_w_sb[:, :], q_w).then_inc(late_loaded, 16)
            sp.dma_start(o_w_sb[:, :, :], o_w).then_inc(late_loaded, 16)
            for i in range(DENSE):
                first = (GATHERED + i) * NK * NK
                sp.dma_start(table_sb[:, i, :, :], kv_table[first:first + NK * NK, :].rearrange("(c p) d -> p c d", p=P)
                             ).then_inc(table_loaded, 16)
            sp.wait_ge(onehot_made, VCHUNKS)
            load_tokens(1)

            def store(tile, at):
                sp.wait_ge(y_ready, tile + 1)
                sp.dma_start(out[at, :], y[:, :]).then_inc(y_stored, 16)
                sp.wait_ge(y_stored, (tile + 1) * 16)
                sp.sem_inc(y_free, 1)

            with nc.Fori(0, ROUNDS, engines=[sp.engine]) as r:
                store(r * PER_ROUND, bass.ds(r * PER_ROUND * P, P))
                with nc.Fori(0, GROUP, engines=[sp.engine]) as b:
                    store(r * PER_ROUND + 1 + b, bass.ds((r * PER_ROUND + 1 + b) * P, P))
            sp.wait_ge(y_stored, 16 * TILES)

        @block.gpsimd
        def _(pool):
            nc.gpsimd.memset(ones[:, :], 1.0)
            nc.gpsimd.memset(eps[:, :], 1e-5)
            nc.gpsimd.iota(vocab_i[:, 0:1], pattern=[[0, 1]], base=0, channel_multiplier=1)
            nc.gpsimd.iota(vocab_i[:, 1:2], pattern=[[0, 1]], base=0, channel_multiplier=1)
            pool.drain()
            nc.gpsimd.iota(vocab_i[P // 2:, 1:2], pattern=[[0, 1]], base=0, channel_multiplier=1)
            pool.drain()
            nc.gpsimd.tensor_copy(vocab_f[:, :], vocab_i[:, :]).then_inc(first_consts_made, 1)
            nc.gpsimd.memset(ident[:, :], 0.0)
            nc.gpsimd.memset(batch_of_row[:, :], 1.0)
            nc.gpsimd.memset(head_blocks[:, :], 1.0 / SEQ)
            nc.gpsimd.memset(patch_mask[:, :], 0.0)
            nc.gpsimd.memset(text_mask[:, :], 0.0)
            nc.gpsimd.memset(batch_window[:, :], NEG)
            nc.gpsimd.memset(spread[:, :, :, :], 0.0)
            nc.gpsimd.iota(key_i[:, :], pattern=[[1, NK]], base=0, channel_multiplier=0)
            nc.gpsimd.iota(place_i[:, :], pattern=[[1, CAND]], base=0, channel_multiplier=0)
            pool.drain()
            nc.gpsimd.memset(batch_window[:, P - PATCHES:P], 0.0)
            nc.gpsimd.affine_select(out=ident[:, :], in_=ident[:, :], compare_op=ALU.not_equal, fill=1.0,
                                    base=0, pattern=[[-1, P]], channel_multiplier=1)

            def keep_block(t, width, fill, per):
                n = t.shape[1] // per
                v = t.rearrange("p (n c) -> p n c", c=per)
                for base, sign in ((0, 1), (width - 1, -1)):
                    nc.gpsimd.affine_select(out=v, in_=v, compare_op=ALU.is_ge, fill=fill, base=base,
                                            pattern=[[-sign * width, n], [0, per]], channel_multiplier=sign)
                    pool.drain()

            keep_block(batch_of_row[:, :], PATCHES, 0.0, 1)
            keep_block(head_blocks[:, :], HC, 0.0, HC)
            keep_block(patch_mask[:, :], PATCHES, NEG, PATCHES)
            for t in (patch_mask[:, :], text_mask[:, :]):
                nc.gpsimd.affine_select(out=t, in_=t, compare_op=ALU.is_ge, fill=NEG,
                                        base=0, pattern=[[-1, P]], channel_multiplier=1)
            nc.gpsimd.tensor_copy(place_f[:, :], place_i[:, :])
            nc.gpsimd.tensor_copy(key_b[:, :], key_i[:, :])
            nc.gpsimd.tensor_copy(ident_b[:, :], ident[:, :])
            flat = spread[:, :, :, :].rearrange("p c j i -> p (c j) i")
            nc.gpsimd.affine_select(out=flat[0:NK], in_=flat[0:NK], compare_op=ALU.not_equal, fill=1.0, base=0,
                                    pattern=[[0, NK], [-1, NK]], channel_multiplier=1)
            pool.drain()
            nc.gpsimd.affine_select(out=flat[NK:P], in_=flat[NK:P], compare_op=ALU.not_equal, fill=1.0, base=0,
                                    pattern=[[-1, NK], [0, NK]], channel_multiplier=1)
            pool.drain()
            nc.gpsimd.memset(x2_t[:, TILES * P:], 0.0).then_inc(consts_made, 1)

            def gather(tile, head):
                slot = head % SLOTS
                if not (isinstance(tile, int) and head < SLOTS):
                    pool.wait_ge(rows_summed, tile * GATHERED + head + 1 - SLOTS)
                wait_apart(pool, rows_ready, tile * GATHERED + head + 1, gathers_begun)
                for k in range(TOP):
                    nc.gpsimd.indirect_dma_start(
                        gathered[:, slot, k, :], None, kv_table,
                        bass.IndirectOffsetOnAxis(rows[:, head, k:k + 1], 0)).then_inc(slot_filled[slot], 16)

            for head in range(GATHERED):
                gather(0, head)
            with nc.Fori(1, TILES, engines=[pool.engine]) as tile:
                for head in range(GATHERED):
                    gather(tile, head)

        @block.scalar
        def _(act):
            act.dma_start(patches_sb[:, :, :], patches).then_inc(patch_loaded, 16)
            act.dma_start(tok_w_sb[:, :, :], tok_w).then_inc(patch_loaded, 16)
            act.dma_start(tok_b_sb[:, :], tok_b.partition_broadcast(P)).then_inc(patch_loaded, 16)
            act.dma_start(vec_sb[:, :, :].rearrange("p a d -> p (a d)"),
                          vectors.partition_broadcast(P)).then_inc(vec_loaded, 16)
            act.dma_start(pk_w_sb[:, :, :], pk_w).then_inc(pk_loaded, 16)
            act.dma_start(pk_keys_sb[:, :, :], pk_keys).then_inc(pk_loaded, 16)

            act.wait_ge(tables_done, 1)
            nc.scalar.copy(projected, bank[2][:, 0:VCHUNKS * D])
            nc.scalar.copy(projected_parts[:, 0, :], bank[2][:, 0:VCHUNKS * D]).then_inc(tables_copied, 1)
            for i in range(2):
                act.wait_ge(fold_done, i + 1)
                nc.scalar.copy(pk_fold[:, i * 512:(i + 1) * 512], bank[i][0:D, :]).then_inc(fold_copied, 1)

            act.wait_ge(consts_made, 1)
            for a in range(TOP):
                last = nc.scalar.mul(ident_ranks[:, a, :], ident_b[:, :], float(TOP - a))
            last.then_inc(ranks_made, 1)

            def front(r):
                for i, (n, scale, bias) in enumerate([(GROUP, 1.0 / D, eps[:, :]), (PER_ROUND, 1.0 / D, eps[:, :]),
                                                      (PER_ROUND * HEADS, 1.0 / (HC - 1), 0.0),
                                                      (PER_ROUND, 1.0 / D, eps[:, :])]):
                    if i == 3:
                        copy_transposed(act, x1_t, 0, r, x1_t_done, x1_t_copied)
                        act.wait_ge(lin_patch_t_done, r + 1)
                        nc.scalar.copy(patch_out_t[:, :], bank[4][0:D, 0:P]).then_inc(lin_patch_t_copied, 1)
                    act.wait_ge(var_ready, 4 * r + i + 1)
                    nc.scalar.activation(std[:, 0:n], var[:, 0:n], ACT.Sqrt, scale=scale,
                                         bias=bias).then_inc(std_ready, 1)
                copy_transposed(act, x2_t, r * PER_ROUND, r, x2_t_done, x2_t_copied)

            def copy_tokens(tile):
                nc.scalar.copy(x2_t_next[:, :], x2_t[:, bass.ds(tile * P, P)]).then_inc(x2_next_ready, 1)

            def copy_scores(tile, half):
                flat = scores[:, :, :, :].rearrange("p h s k -> p (h s k)")
                act.wait_ge(scores_done, 2 * tile + half + 1)
                nc.scalar.copy(flat[:, half * 512:(half + 1) * 512],
                               bank[0 if half else 5][:, :]).then_inc(scores_copied, 1)

            def copy_queries(tile):
                act.wait_ge(q_done, tile + 1)
                nc.scalar.mul(q_t[:, :, :].rearrange("p a b -> p (a b)"), bank[1][:, :], D ** -0.5).then_inc(q_copied, 1)

            def weigh_rows(tile, head, lo=0, hi=TOP):
                slot = head % SLOTS
                if lo == 0:
                    act.wait_ge(slot_filled[slot], (tile * (GATHERED // SLOTS) + head // SLOTS + 1) * TOP * 16)
                for k in range(lo, hi):
                    nc.scalar.mul(gathered[:, slot, k, :], gathered[:, slot, k, :],
                                  weight[:, head, k:k + 1]).then_inc(rows_weighted, 1)

            def weigh(tile, head):
                act.wait_ge(best_ready, tile * HEADS + SEARCHED.index(head) + 1)
                nc.scalar.activation(weight[:, head, :], best[:, head, :], ACT.Exp, bias=neg_best[:, head:head + 1],
                                     accum_out=weight_sum[:, head:head + 1]).then_inc(weight_ready, 1)

            def scale_hot(nth, lo=0, hi=TOP):
                if lo == 0:
                    act.wait_ge(hot_marked, nth + 1)
                for a in range(lo, hi):
                    end = nc.scalar.mul(hot[:, a, 0:NK], hot[:, a, 0:NK], row_count[:, a:a + 1])
                if hi == TOP:
                    end.then_inc(hot_ready, 1)

            def copy_turned(tile, i):
                act.wait_ge(turned_done, tile * DENSE + i + 1)
                nc.scalar.copy(reach_t[:, i, :], bank[3][:, 0:P])
                nc.scalar.copy(score_t[:, :], bank[3][:, P:2 * P])
                nc.scalar.copy(score_parts[:, i, 0, :], bank[3][:, P:2 * P]).then_inc(turned_copied, 1)

            def grid_exps(tile, groups, rows=None, ranks=None):
                def share(lo, hi, n):
                    return lo + (hi - lo) * n // len(groups), lo + (hi - lo) * (n + 1) // len(groups)

                for n, g in enumerate(groups):
                    act.wait_ge(grid_scored, tile * DENSE * GROUPS + g + 1)
                    nc.scalar.activation(grid_exp[:, g % 2, :], grid[g % 2][:, 0:2 * P], ACT.Exp).then_inc(grid_expd, 1)
                    if rows:
                        weigh_rows(rows[0], rows[1], *share(rows[2], rows[3], n))
                    if ranks:
                        scale_hot(ranks[0], *share(ranks[1], ranks[2], n))

            front(0)
            act.wait_ge(x2_t_copied, QUADS)
            copy_tokens(0)
            copy_scores(0, 0)
            copy_scores(0, 1)
            copy_tokens(1)
            for head in SEARCHED:
                weigh(0, head)
                if head == GATHERED:
                    scale_hot(0)
                    copy_turned(0, 0)
                if head == 3:
                    copy_scores(1, 0)
            copy_queries(0)
            grid_exps(0, [0, 1])
            weigh_rows(0, 0)
            weigh_rows(0, 1)

            def tile_step(tile, text, last=False):
                k_t = k_t_text if text else k_t_patch
                width = 2 * P if text else P

                def turn_keys(j):
                    act.wait_ge(k_t_done, tile * 4 + PAIR_ORDER.index(j) + 1)
                    nc.scalar.copy(k_t[:, j, :], bank[3][:, j * P:(j + 1) * P]).then_inc(k_t_copied, 1)

                def exp_pair(j):
                    for head in (2 * j, 2 * j + 1):
                        act.wait_ge(max_ready, tile * HEADS + nth_head(head) + 1)
                        nc.scalar.activation(prob[:, head % 2, 0:width], sim[head % 2][:, 0:width], ACT.Exp,
                                             bias=neg_max[:, head:head + 1],
                                             accum_out=prob_sum[:, head:head + 1]).then_inc(prob_ready, 1)

                def copy_pair(j):
                    for head in (2 * j, 2 * j + 1):
                        act.wait_ge(prob_t_done, tile * HEADS + nth_head(head) + 1)
                        nc.scalar.copy(prob_t[:, head % 2, 0:width],
                                       turned[j][head % 2][:, 0:width]).then_inc(prob_t_copied, 1)

                grid_exps(tile, SCORED[0], (tile, 2, 0, TOP), (tile * DENSE + 1, 0, 10))
                if not last:
                    weigh(tile + 1, 0)
                grid_exps(tile, SCORED[1][:3], (tile, 3, 0, 9), (tile * DENSE + 1, 10, TOP))
                copy_turned(tile, 1)
                if not last:
                    copy_scores(tile + 1, 1)
                grid_exps(tile, SCORED[1][3:4], (tile, 3, 9, 12))
                turn_keys(0)
                grid_exps(tile, SCORED[1][4:], (tile, 3, 12, TOP))
                exp_pair(0)
                grid_exps(tile, SCORED[2][:1], (tile, 4, 0, 2))
                copy_pair(0)
                if not last:
                    weigh(tile + 1, 1)
                grid_exps(tile, SCORED[2][1:], (tile, 4, 2, 10))
                grid_exps(tile, SCORED[GATHERED], (tile, 4, 10, TOP))
                if last:
                    grid_exps(tile, SCORED[3][:2])
                    turn_keys(1)
                    grid_exps(tile, SCORED[3][2:])
                else:
                    weigh(tile + 1, 2)
                    weigh(tile + 1, GATHERED)
                    ranks = (tile + 1) * DENSE
                    grid_exps(tile, SCORED[3][:2], (tile, 5, 0, 5), (ranks, 0, 4))
                    turn_keys(1)
                    grid_exps(tile, SCORED[3][2:], (tile, 5, 5, TOP), (ranks, 4, 12))
                if last:
                    exp_pair(1)
                    grid_exps(tile, SCORED[4][:1])
                    copy_pair(1)
                    grid_exps(tile, SCORED[4][1:])
                else:
                    weigh(tile + 1, 3)
                    exp_pair(1)
                    grid_exps(tile, SCORED[4][:1], (tile + 1, 0, 0, 2), (ranks, 12, TOP))
                    copy_pair(1)
                    grid_exps(tile, SCORED[4][1:3], (tile + 1, 0, 2, 8))
                    copy_turned(tile + 1, 0)
                    grid_exps(tile, SCORED[4][3:], (tile + 1, 0, 8, 12))
                    copy_tokens(tile + 2)
                    weigh_rows(tile + 1, 0, 12, TOP)
                turn_keys(DENSE_PAIR)
                if last:
                    exp_pair(DENSE_PAIR)
                    copy_pair(DENSE_PAIR)
                    weigh_rows(tile, 5)
                    turn_keys(LAST_PAIR)
                else:
                    turn_keys(LAST_PAIR)
                    exp_pair(DENSE_PAIR)
                    copy_pair(DENSE_PAIR)
                    weigh(tile + 1, 4)
                    weigh_rows(tile + 1, 1, 0, 8)
                exp_pair(LAST_PAIR)
                if not last:
                    copy_scores(tile + 2, 0)
                copy_pair(LAST_PAIR)
                if not last:
                    copy_queries(tile + 1)
                    weigh_rows(tile + 1, 1, 8, TOP)
                act.wait_ge(at_t_done, tile + 1)
                nc.scalar.copy(attended_t[:, :, :].rearrange("p a b -> p (a b)"), bank[3][:, :]).then_inc(at_t_copied, 1)
                if not last:
                    weigh(tile + 1, 5)
                    grid_exps(tile + 1, [0, 1])
                    weigh(tile + 1, GATHERED + 1)

            for r in range(ROUNDS):
                tile_step(r * PER_ROUND, False)
                for lo, hi in BATCH_RUNS[r]:
                    with nc.Fori(lo, hi, engines=[act.engine]) as b:
                        tile_step(r * PER_ROUND + 1 + b, True)
                    if (r, hi) == NEXT_FRONT:
                        front(r + 1)
                        act.wait_ge(x2_t_copied, (r + 2) * QUADS)
            tile_step(TILES - 1, True, last=True)

        @block.tensor
        def _(pe):
            mm = nc.tensor.matmul
            pe.wait_ge(first_consts_made, 1)
            pe.wait_ge(w_summed, 1)
            mm(bank[7][0:EMB, 0:1], ones[0:EMB, 0:EMB], w_stat[:, 0:1], start=True, stop=True).then_inc(w_total, 1)
            pe.wait_ge(w_made, 1)
            for c in range(VCHUNKS):
                last = mm(bank[2][:, c * D:(c + 1) * D], tables_sb[:, c, :], w_eff[:, :], start=True, stop=True)
            last.then_inc(tables_done, 1)
            pe.wait_ge(tables_copied, 1)
            pe.wait_ge(pk_loaded, 32)
            for half in range(2):
                for i in range(HEADS):
                    u = half * HEADS + i
                    last = mm(bank[half][0:D, i * NK:(i + 1) * NK], pk_w_sb[:, u, :], pk_keys_sb[:, u, :],
                              start=True, stop=True)
                last.then_inc(fold_done, 1)

            pe.wait_ge(patch_loaded, 48)
            for r in range(ROUNDS):
                for c in range(KPATCH):
                    last = mm(bank[3][:, r * D:(r + 1) * D], patches_sb[:, c, r * P:(r + 1) * P],
                              tok_w_sb[:, c, :], start=(c == 0), stop=(c == KPATCH - 1))
            last.then_inc(patch_embedded, 1)
            def transpose_tiles(src, r, done, copied):
                for g in range(QUADS):
                    if g >= 2:
                        pe.wait_ge(copied, r * QUADS + g - 1)
                    for i in range(min(4, PER_ROUND - 4 * g)):
                        last = nc.tensor.transpose(bank[5 + g % 2][0:D, i * P:(i + 1) * P],
                                                   src[:, 4 * g + i, :], ident[:, :])
                    last.then_inc(done, 1)

            def front(r):
                pe.wait_ge(onehot_made, (r + 1) * VCHUNKS)
                pe.wait_ge(projected_split, 1)
                for b in range(GROUP):
                    for c in range(VCHUNKS):
                        for part in range(3):
                            last = mm(bank[4][:, b * D:(b + 1) * D], onehot[:, c, b * P:(b + 1) * P],
                                      projected_parts[:, part, c * D:(c + 1) * D],
                                      start=(c == 0 and part == 0), stop=(c == VCHUNKS - 1 and part == 2))
                last.then_inc(text_embedded, 1)
                pe.wait_ge(x1_ready, r + 1)
                transpose_tiles(x1, r, x1_t_done, x1_t_copied)
                pe.wait_ge(kv1_in, r + 1)
                mm(bank[3][0:D, :], k1[:, 0, :], v1_split[:, :, :].rearrange("p b d -> p (b d)"),
                   start=True, stop=False, skip_group_check=True)
                for b in range(GROUP):
                    last = mm(bank[3][0:D, b * D:(b + 1) * D], k1[:, 1 + b, :], v1[:, 1 + b, :],
                              start=False, stop=(b == GROUP - 1), skip_group_check=True)
                last.then_inc(kv1_done, 1)
                pe.wait_ge(kv1_ready, r + 1)
                pe.wait_ge(x1_t_copied, (r + 1) * QUADS)
                for b in range(GROUP):
                    last = mm(bank[4][0:D, b * PATCHES:(b + 1) * PATCHES], kv1[:, b, :],
                              x1_t[:, b * PATCHES:(b + 1) * PATCHES], start=True, stop=True)
                last.then_inc(lin_patch_t_done, 1)
                for b in range(GROUP):
                    last = mm(bank[0][:, b * D:(b + 1) * D], x1_t[:, (1 + b) * P:(2 + b) * P], kv1[:, b, :],
                              start=True, stop=True)
                last.then_inc(lin_text_done, 1)
                pe.wait_ge(lin_patch_t_copied, r + 1)
                nc.tensor.transpose(bank[4][:, P:P + D], patch_out_t[:, :], ident[0:D, 0:D]).then_inc(lin_patch_done, 1)
                pe.wait_ge(x2_ready, r + 1)
                transpose_tiles(x2, r, x2_t_done, x2_t_copied)
                pe.wait_ge(x2_t_copied, (r + 1) * QUADS)

            def score(tile, half):
                if half == 0:
                    pe.wait_ge(x2_next_ready, tile + 1)
                nc.tensor.matmul(bank[0 if half else 5][:, :], x2_t_next[:, :], pk_fold[:, half * 512:(half + 1) * 512],
                                 start=True, stop=True).then_inc(scores_done, 1)

            pe.wait_ge(fold_copied, 2)
            front(0)
            def turn(tile, i):
                pe.wait_ge(hot_ready, tile * DENSE + i + 1)
                for a in range(TOP):
                    mm(bank[3][0:NK, 0:P], hot[:, a, 0:NK], ident_b[:, :], start=(a == 0), stop=(a == TOP - 1))
                for a in range(TOP):
                    mm(bank[3][NK:P, 0:P], hot[:, a, NK:P], ident_ranks[:, a, :], start=(a == 0), stop=(a == TOP - 1))
                nc.tensor.transpose(bank[3][:, P:2 * P],
                                    scores[:, GATHERED + i, :, :].rearrange("p s k -> p (s k)"),
                                    ident[:, :]).then_inc(turned_done, 1)

            def sum_rows(tile, head, lo=0, hi=TOP):
                if lo == 0 and head == 0:
                    pe.wait_ge(q_copied, tile + 1)
                if lo == 0 and head > 0:
                    pe.wait_ge(kv_copied, tile * GATHERED + head)
                for k in range(lo, hi):
                    if k % 4 == 0:
                        pe.wait_ge(rows_weighted, (tile * GATHERED + head) * TOP + k + 4)
                    last = mm(bank[1][:, 0:P], ident[:, :], gathered[:, head % SLOTS, k, :],
                              start=(k == 0), stop=(k == TOP - 1))
                if hi == TOP:
                    last.then_inc(rows_summed, 1)

            def queries(tile):
                if not isinstance(tile, int) or tile > 0:
                    pe.wait_ge(kv_copied, tile * GATHERED)
                for j in range(4):
                    end = mm(bank[1][:, j * P:(j + 1) * P], q_w_sb[:, j * P:(j + 1) * P],
                             x2_t[:, bass.ds(tile * P, P)], start=True, stop=True)
                end.then_inc(q_done, 1)

            def score_group(tile, g):
                i = g // GROUPS
                base = tile * DENSE * GROUPS
                if g >= 2:
                    pe.wait_ge(grid_masked, base + g - 1)
                for c in range(2):
                    pick = spread[:, 2 * (g % GROUPS) + c, :, :].rearrange("p j i -> p (j i)")
                    for part in range(3):
                        mm(grid[g % 2][:, c * P:(c + 1) * P], pick, score_parts[:, i, part, :],
                           start=(part == 0), stop=(part == 2))
                    end = mm(grid[g % 2][:, (2 + c) * P:(3 + c) * P], pick, reach_t[:, i, :], start=True, stop=True)
                end.then_inc(grid_scored, 1)

            def mix_group(tile, g):
                i = g // GROUPS
                pe.wait_ge(grid_masked, tile * DENSE * GROUPS + g + 1)
                if g == GROUPS:
                    pe.wait_ge(dense_copied, tile * DENSE + 1)
                for c in range(2):
                    at = g % GROUPS * 2 + c
                    end = mm(bank[5][:, 0:P], grid_w[:, g % 2, c * P:(c + 1) * P], table_sb[:, i, at, :],
                             start=(at == 0), stop=(at == CHUNKS - 1))
                end.then_inc(dense_done if g % GROUPS == GROUPS - 1 else grid_mixed, 1)

            def dense_groups(tile, groups, head=None, lo=0):
                for n, g in enumerate(groups):
                    if g % GROUPS == 0:
                        pe.wait_ge(parts_ready, tile * DENSE + g // GROUPS + 1)
                    score_group(tile, g)
                    if g >= 2:
                        mix_group(tile, g - 2)
                    if head is not None and lo + 4 * n < TOP:
                        sum_rows(tile, head, lo + 4 * n, lo + 4 * n + 4)

            score(0, 0)
            score(0, 1)
            pe.wait_ge(ranks_made, 1)
            pe.wait_ge(scores_copied, 1)
            score(1, 0)
            turn(0, 0)
            pe.wait_ge(late_loaded, 32)
            queries(0)
            dense_groups(0, [0, 1])
            pe.wait_ge(q_copied, 1)
            sum_rows(0, 0)
            pe.wait_ge(table_loaded, 16 * DENSE)

            def tile_step(tile, text, b, last=False):
                kv, k_t = (kv_text, k_t_text) if text else (kv_patch, k_t_patch)
                keys = ([k_t_patch] if text else []) + [k_t]
                vals = ([kv_patch] if text else []) + [kv]
                masks = [batch_window[:, bass.ds((GROUP - 1) * PATCHES - b * PATCHES, P)],
                         text_mask[:, :]] if text else [patch_mask[:, :]]

                def turn_keys(j):
                    if 2 * j < GATHERED:
                        pe.wait_ge(kv_copied, tile * GATHERED + 2 * j + 2)
                    else:
                        pe.wait_ge(dense_copied, (tile + 1) * DENSE)
                    nc.tensor.transpose(bank[3][:, j * P:(j + 1) * P],
                                        kv[:, 0, 2 * j:2 * j + 2, :].rearrange("p a d -> p (a d)"),
                                        ident[:, :]).then_inc(k_t_done, 1)

                def compare(j):
                    pe.wait_ge(k_t_copied, tile * 4 + PAIR_ORDER.index(j) + 1)
                    for head in (2 * j, 2 * j + 1):
                        lo = (head % 2) * D
                        for n, (key, mask) in enumerate(zip(keys, masks)):
                            part = sim[head % 2][:, n * P:(n + 1) * P]
                            mm(part, q_t[lo:lo + D, j, :], key[lo:lo + D, j, :], start=True, stop=False)
                            end = mm(part, ident[:, :], mask, start=False, stop=True)
                        end.then_inc(sim_done, 1)

                def turn_pair(j):
                    pe.wait_ge(prob_ready, tile * HEADS + nth_head(2 * j + 1) + 1)
                    for head in (2 * j, 2 * j + 1):
                        for n in range(len(keys)):
                            end = nc.tensor.transpose(turned[j][head % 2][:, n * P:(n + 1) * P],
                                                      prob[:, head % 2, n * P:(n + 1) * P], ident[:, :])
                        end.then_inc(prob_t_done, 1)

                def mix_pair(j):
                    for head in (2 * j, 2 * j + 1):
                        pe.wait_ge(prob_t_copied, tile * HEADS + nth_head(head) + 1)
                        for n, val in enumerate(vals):
                            end = mm(bank[6][:, head * D:(head + 1) * D], prob_t[:, head % 2, n * P:(n + 1) * P],
                                     val[:, 1, head, :], start=(n == 0), stop=(n == len(vals) - 1))
                        end.then_inc(av_done, 1)

                dense_groups(tile, SCORED[0], 1)
                dense_groups(tile, SCORED[1][:3], 2)
                turn(tile, 1)
                if not last:
                    score(tile + 1, 1)
                dense_groups(tile, SCORED[1][3:4], 2, 12)
                pe.wait_ge(turned_copied, (tile + 1) * DENSE)
                turn_keys(0)
                dense_groups(tile, SCORED[1][4:])
                if not last:
                    pe.wait_ge(scores_copied, 2 * tile + 4)
                compare(0)
                dense_groups(tile, SCORED[2][:1], 3)
                turn_pair(0)
                dense_groups(tile, SCORED[2][1:3], 3, 4)
                mix_pair(0)
                dense_groups(tile, SCORED[2][3:], 3, 12)
                dense_groups(tile, SCORED[GATHERED])
                dense_groups(tile, SCORED[3][:2], 4)
                turn_keys(1)
                dense_groups(tile, SCORED[3][2:], 4, 8)
                compare(1)
                rows_of = None if last else 5
                dense_groups(tile, SCORED[4][:1], rows_of)
                turn_pair(1)
                dense_groups(tile, SCORED[4][1:3], rows_of, 4)
                if not last:
                    turn(tile + 1, 0)
                dense_groups(tile, SCORED[4][3:], rows_of, 12)
                mix_pair(1)
                for g in (DENSE * GROUPS - 2, DENSE * GROUPS - 1):
                    mix_group(tile, g)
                if not last:
                    pe.wait_ge(turned_copied, (tile + 1) * DENSE + 1)
                turn_keys(DENSE_PAIR)
                compare(DENSE_PAIR)
                if last:
                    turn_pair(DENSE_PAIR)
                    mix_pair(DENSE_PAIR)
                    sum_rows(tile, 5)
                    turn_keys(LAST_PAIR)
                    compare(LAST_PAIR)
                else:
                    turn_keys(LAST_PAIR)
                    turn_pair(DENSE_PAIR)
                    compare(LAST_PAIR)
                    mix_pair(DENSE_PAIR)
                    score(tile + 2, 0)
                turn_pair(LAST_PAIR)
                if not last:
                    queries(tile + 1)
                mix_pair(LAST_PAIR)
                if not last:
                    sum_rows(tile + 1, 0, 0, 8)
                pe.wait_ge(av_scaled, tile + 1)
                for j in range(4):
                    end = nc.tensor.transpose(bank[3][:, j * P:(j + 1) * P], attended[:, j * P:(j + 1) * P], ident[:, :])
                end.then_inc(at_t_done, 1)
                if not last:
                    dense_groups(tile + 1, [0, 1])
                pe.wait_ge(at_t_copied, tile + 1)
                for j in range(4):
                    end = mm(bank[4][:, 0:D], attended_t[:, j, :], o_w_sb[:, j, :], start=(j == 0), stop=(j == 3))
                end.then_inc(y_done, 1)
                if not last:
                    sum_rows(tile + 1, 0, 8, TOP)
            for r in range(ROUNDS):
                tile_step(r * PER_ROUND, False, None)
                for lo, hi in BATCH_RUNS[r]:
                    with nc.Fori(lo, hi, engines=[pe.engine]) as b:
                        tile_step(r * PER_ROUND + 1 + b, True, b)
                    if (r, hi) == NEXT_FRONT:
                        front(r + 1)
            tile_step(TILES - 1, True, GROUP - 1, last=True)

        @block.vector
        def _(dve):
            v = nc.vector
            done = dve.drain

            dve.wait_ge(txt_w_loaded, 32)
            v.tensor_reduce(w_stat[:, 0:1], txt_w_sb[:, :], X, ALU.add, apply_absolute_value=True).then_inc(w_summed, 1)
            dve.wait_ge(first_consts_made, 1)

            def split(whole, rests, parts):
                v.tensor_tensor(rests[0], whole, parts[0], ALU.subtract)
                done()
                v.tensor_copy(parts[1], rests[0])
                done()
                v.tensor_tensor(rests[1], rests[0], parts[1], ALU.subtract)
                done()
                return v.tensor_copy(parts[2], rests[1])

            def pick_columns(c):
                column = vocab_f[:, 1:2] if c in (0, 3) else vocab_f[:, 0:1]
                v.tensor_scalar(onehot[:, c, :], tokens_sb[:, c, :], column, None,
                                ALU.is_equal).then_inc(onehot_made, 1)

            dve.wait_ge(w_total, 1)
            v.tensor_scalar(w_stat[:, 1:2], bank[7][0:EMB, 0:1], 1.0 / (EMB * D), None, ALU.mult)
            done()
            v.tensor_scalar(w_stat[:, 2:3], w_stat[:, 1:2], 1e-8, None, ALU.add)
            done()
            v.reciprocal(w_stat[:, 3:4], w_stat[:, 2:3])
            done()
            v.tensor_scalar(w_eff[:, :], txt_w_sb[:, :], w_stat[:, 3:4], None, ALU.mult)
            done()
            v.tensor_scalar(w_eff[:, :], w_eff[:, :], 1.0, -1.0, ALU.min, ALU.max)
            done()
            v.tensor_scalar(w_eff[:, :], w_eff[:, :], MAGIC, None, ALU.add)
            done()
            v.tensor_scalar(w_eff[:, :], w_eff[:, :], MAGIC, None, ALU.subtract)
            done()
            v.scalar_tensor_tensor(w_eff[:, :], w_eff[:, :], w_stat[:, 1:2], txt_w_sb[:, :],
                                   ALU.mult, ALU.subtract)
            done()
            v.tensor_tensor(w_eff[:, :], w_eff[:, :], txt_w_sb[:, :], ALU.add).then_inc(w_made, 1)
            dve.wait_ge(tokens_loaded[0], 6 * 16)
            for c in range(VCHUNKS):
                pick_columns(c)
            dve.wait_ge(tables_copied, 1)
            split(projected, [projected_rest[:, i, :] for i in range(2)],
                  [projected_parts[:, i, :] for i in range(3)]).then_inc(projected_split, 1)
            dve.wait_ge(consts_made, 1)
            v.tensor_scalar(place_f[:, :], place_f[:, :], float(PLACE), None, ALU.mult)
            dve.wait_ge(patch_loaded, 48)
            dve.wait_ge(patch_embedded, 1)
            v.tensor_tensor(h[:, 0:TILES:PER_ROUND, :], bank[3][:, 0:ROUNDS * D].rearrange("p (r d) -> p r d", d=D),
                            tok_b_sb[:, :].unsqueeze(1).to_broadcast([P, ROUNDS, D]), ALU.add)
            dve.wait_ge(vec_loaded, 16)

            n_std = [0]

            def normalise(parts, groups, width, signal=None):
                at = 0
                for src, cen, squ, _ in parts:
                    n = src.shape[1]
                    v.tensor_reduce(mean[:, at:at + n], src, X, ALU.add)
                    at += n
                done()
                v.tensor_scalar(mean[:, 0:at], mean[:, 0:at], 1.0 / width, None, ALU.mult)
                done()
                at = 0
                for src, cen, squ, _ in parts:
                    n = src.shape[1]
                    v.tensor_tensor(cen, src, over(mean[:, at:at + n], [P, n, width]), ALU.subtract)
                    at += n
                done()
                for src, cen, squ, _ in parts:
                    v.tensor_tensor(squ, cen, cen, ALU.mult)
                done()
                at = 0
                for src, cen, squ, _ in parts:
                    n = src.shape[1]
                    last = v.tensor_reduce(var[:, at:at + n], squ, X, ALU.add)
                    at += n
                last.then_inc(var_ready, 1)
                n_std[0] += 1
                dve.wait_ge(std_ready, n_std[0])
                if groups == "heads":
                    v.tensor_scalar(std[:, 0:at], std[:, 0:at], 1e-5, None, ALU.add)
                    done()
                v.reciprocal(std[:, 0:at], std[:, 0:at])
                done()
                at = 0
                for src, cen, squ, dst in parts:
                    n = src.shape[1]
                    last = v.tensor_tensor(dst, cen, over(std[:, at:at + n], [P, n, width]), ALU.mult)
                    at += n
                if signal is not None:
                    last.then_inc(signal, 1)
                done()

            def front(r):
                t = r * PER_ROUND

                def tiles(a):
                    return a[:, t:t + PER_ROUND, :] if a is h else a[:, :, :]

                def text_tiles(a):
                    return a[:, t + 1:t + PER_ROUND, :] if a is h else a[:, 1:PER_ROUND, :]

                dve.wait_ge(text_embedded, r + 1)
                v.tensor_tensor(text_tiles(h), bank[4][:, :].rearrange("p (b d) -> p b d", d=D),
                                vec("b", GROUP), ALU.add)
                done()
                normalise([tuple(text_tiles(a) for a in (h, dev, sq, h))], "rows", D)
                for name, op in (("gamma", ALU.mult), ("beta", ALU.add)):
                    v.tensor_tensor(text_tiles(h), text_tiles(h), vec(name, GROUP), op)
                    done()
                normalise([tuple(tiles(a) for a in (h, dev, sq, x1))], "rows", D, x1_ready)
                normalise([tuple(tiles(a).rearrange("p t (h c) -> p (t h) c", c=HC) for a in (x1, dev, sq, dev))],
                          "heads", HC)
                for a, w in ((k1, "k_w"), (v1, "v_w")):
                    v.tensor_tensor(tiles(a), tiles(dev), vec(w, PER_ROUND), ALU.mult)
                done()
                for a, w in ((k1, "k_b"), (v1, "v_b")):
                    v.tensor_tensor(tiles(a), tiles(a), vec(w, PER_ROUND), ALU.add)
                done()
                v.tensor_tensor(v1_split[:, :, :], v1[:, 0:1, :].to_broadcast([P, GROUP, D]),
                                over(batch_of_row[:, :], [P, GROUP, D]), ALU.mult).then_inc(kv1_in, 1)
                v.tensor_tensor(tiles(h), tiles(h), tiles(x1), ALU.add)
                dve.wait_ge(kv1_done, r + 1)
                v.tensor_tensor(kv1[:, :, :], bank[3][0:D, :].rearrange("p (b d) -> p b d", d=D),
                                head_blocks[:, :].unsqueeze(1).to_broadcast([D, GROUP, D]),
                                ALU.mult).then_inc(kv1_ready, 1)
                done()
                dve.wait_ge(lin_text_done, r + 1)
                v.tensor_tensor(text_tiles(h), text_tiles(h), bank[0][:, :].rearrange("p (b d) -> p b d", d=D), ALU.add)
                dve.wait_ge(lin_patch_done, r + 1)
                v.tensor_tensor(h[:, t, :], h[:, t, :], bank[4][:, P:P + D], ALU.add)
                done()
                normalise([tuple(tiles(a) for a in (h, dev, sq, x2))], "rows", D, x2_ready)

            v.memset(y[:, :], 0.0).then_inc(y_free, 1)
            done()

            def mask_group(tile, g):
                dve.wait_ge(grid_expd, tile * DENSE * GROUPS + g + 1)
                if g % GROUPS >= 2:
                    dve.wait_ge(grid_mixed, tile * DENSE * (GROUPS - 1) + g // GROUPS * (GROUPS - 1) + g % GROUPS - 1)
                v.scalar_tensor_tensor(grid_w[:, g % 2, :], grid[g % 2][:, 2 * P:4 * P], float(TOP),
                                       grid_exp[:, g % 2, :], ALU.is_gt, ALU.mult).then_inc(grid_masked, 1)

            def split_scores(tile, i):
                dve.wait_ge(turned_copied, tile * DENSE + i + 1)
                split(score_t[:, :], [score_rest[:, n, :] for n in range(2)],
                      [score_parts[:, i, n, :] for n in range(3)]).then_inc(parts_ready, 1)

            def step(now, groups, n):
                done()
                if n < len(groups):
                    mask_group(now, groups[n])

            def best_keys(tile, head, now, groups):
                if head == 0:
                    wait_apart(dve, scores_copied, 2 * tile + 1, searches_begun)
                if head == GATHERED:
                    wait_apart(dve, scores_copied, 2 * tile + 2, searches_begun)
                both = range(2)
                src = [scores[:, head, s, :] for s in both]
                for s in both:
                    v.max(half_top[:, s, 0:8], src[s])
                step(now, groups, 0)
                for s in both:
                    v.max_index(half_idx[:, s, 0:8], half_top[:, s, 0:8], src[s])
                    v.match_replace(rest[:, s, :], half_top[:, s, 0:8], src[s], DROPPED)
                done()
                for s in both:
                    v.max(half_top[:, s, 8:16], rest[:, s, :])
                step(now, groups, 1)
                for s in both:
                    v.max_index(half_idx[:, s, 8:16], half_top[:, s, 8:16], rest[:, s, :])
                done()
                if head >= GATHERED:
                    v.tensor_copy(half_idx_f[:, :, :], half_idx[:, :, :])
                else:
                    v.tensor_scalar(half_key[:, 0, :], half_idx[:, 0, :], float(head * NK * NK), None, ALU.add)
                    v.tensor_scalar(half_key[:, 1, :], half_idx[:, 1, :], float(NK), None, ALU.mult)
                    done()

            def best_pairs(tile, head, now, groups):
                dense = head >= GATHERED
                for dst, half in ((cand, half_top), (cand_row, half_key))[:1 if dense else 2]:
                    at = 0
                    for a, n, cols in BLOCKS:
                        v.tensor_tensor(dst[:, at:at + n * cols].rearrange("p (a b) -> p a b", b=cols),
                                        half[:, 0, a:a + n].unsqueeze(2).to_broadcast([P, n, cols]),
                                        half[:, 1:2, 0:cols].to_broadcast([P, n, cols]), ALU.add)
                        at += n * cols
                step(now, groups, 0)
                v.max(best[:, head, 0:8], cand[:, :])
                if not dense:
                    v.tensor_tensor(cand_row[:, :], cand_row[:, :], place_f[:, :], ALU.add)
                done()
                if not dense:
                    v.max_index(best_at[:, 0:8], best[:, head, 0:8], cand[:, :])
                v.match_replace(cand_rest[:, :], best[:, head, 0:8], cand[:, :], DROPPED)
                step(now, groups, 1)
                v.max(best[:, head, 8:16], cand_rest[:, :])
                v.tensor_scalar(neg_best[:, head:head + 1], best[:, head, 0:1], -1.0, None, ALU.mult).then_inc(best_ready, 1)
                done()

            def find_rows(tile, head, now, groups):
                v.max_index(best_at[:, 8:16], best[:, head, 8:16], cand_rest[:, :])
                done()
                v.tensor_scalar(best_place[:, :], best_at[:, :], float(PLACE), None, ALU.mult)
                done()
                v.tensor_tensor(picked[:, :, :], cand_row[:, :].unsqueeze(1).to_broadcast([P, TOP, CAND]),
                                over(best_place[:, :], [P, TOP, CAND]), ALU.subtract)
                step(now, groups, 0)
                v.tensor_reduce(best_row[:, :], picked[:, :, :], X, ALU.min, apply_absolute_value=True)
                step(now, groups, 1)
                v.tensor_copy(rows[:, head, :], best_row[:, :]).then_inc(rows_ready, 1)

            def mark_pairs(tile, head, now, groups):
                v.match_replace(chosen[:, :], best[:, head, 8:16], cand_rest[:, :], DROPPED)
                v.tensor_scalar(scores[:, head, 0, :], scores[:, head, 0, :], neg_best[:, head:head + 1], None, ALU.add)
                done()
                v.tensor_tensor(chosen[:, :], chosen[:, :], cand[:, :], ALU.not_equal)
                done()
                at = 0
                for a, n, cols in BLOCKS:
                    v.tensor_reduce(row_count[:, a:a + n],
                                    chosen[:, at:at + n * cols].rearrange("p (a b) -> p a b", b=cols), X, ALU.add)
                    at += n * cols
                done()
                for half in range(2):
                    if half < len(groups):
                        mask_group(now, groups[half])
                    end = v.tensor_tensor(hot[:, :, half * NK:(half + 1) * NK],
                                          key_b[:, :].unsqueeze(1).to_broadcast([P, TOP, NK]),
                                          over(half_idx_f[:, half, :], [P, TOP, NK]), ALU.is_equal)
                end.then_inc(hot_marked, 1)

            def search(tile, head, now=None, groups=()):
                best_keys(tile, head, now, groups[0:2])
                best_pairs(tile, head, now, groups[2:4])
                if head < GATHERED:
                    find_rows(tile, head, now, groups[4:6])
                else:
                    mark_pairs(tile, head, now, groups[4:6])

            def take_rows(tile, head, kv):
                dve.wait_ge(rows_summed, tile * GATHERED + head + 1)
                v.reciprocal(weight_inv[:, head:head + 1], weight_sum[:, head:head + 1])
                done()
                v.tensor_scalar(kv[:, :, head, :], bank[1][:, 0:P].rearrange("p (s d) -> p s d", d=D),
                                weight_inv[:, head:head + 1], None, ALU.mult).then_inc(kv_copied, 1)

            def take_dense(tile, i, kv):
                head = GATHERED + i
                dve.wait_ge(dense_done, tile * DENSE + i + 1)
                v.reciprocal(weight_inv[:, head:head + 1], weight_sum[:, head:head + 1])
                done()
                v.tensor_scalar(kv[:, :, head, :], bank[5][:, 0:P].rearrange("p (s d) -> p s d", d=D),
                                weight_inv[:, head:head + 1], None, ALU.mult).then_inc(dense_copied, 1)

            front(0)
            for head in SEARCHED:
                if head == GATHERED + 1:
                    split_scores(0, 0)
                search(0, head)

            def next_front(r):
                dve.wait_ge(tokens_loaded[r], 6 * 16)
                for c in range(VCHUNKS):
                    pick_columns(c)
                front(r)

            def tile_step(tile, text, b, last=False):
                kv = kv_text if text else kv_patch
                width = 2 * P if text else P

                def attend(j):
                    for head in (2 * j, 2 * j + 1):
                        dve.wait_ge(sim_done, tile * HEADS + nth_head(head) + 1)
                        v.tensor_reduce(neg_max[:, head:head + 1], sim[head % 2][:, 0:width], X, ALU.max,
                                        negate=True).then_inc(max_ready, 1)

                def search_next(head):
                    if last:
                        for g in MASKED[head]:
                            mask_group(tile, g)
                    else:
                        search(tile + 1, head, tile, MASKED[head])

                take_rows(tile, 0, kv)
                search_next(0)
                take_rows(tile, 1, kv)
                search_next(1)
                split_scores(tile, 1)
                take_rows(tile, 2, kv)
                attend(0)
                search_next(2)
                take_dense(tile, 0, kv)
                search_next(GATHERED)
                take_rows(tile, 3, kv)
                search_next(3)
                take_rows(tile, 4, kv)
                attend(1)
                search_next(4)
                if not last:
                    split_scores(tile + 1, 0)
                take_dense(tile, 1, kv)
                if last:
                    attend(DENSE_PAIR)
                    take_rows(tile, 5, kv)
                else:
                    take_rows(tile, 5, kv)
                    best_keys(tile + 1, 5, tile, [])
                    attend(DENSE_PAIR)
                    best_pairs(tile + 1, 5, tile, [])
                    find_rows(tile + 1, 5, tile, [])
                attend(LAST_PAIR)
                if not last:
                    best_keys(tile + 1, GATHERED + 1, tile, [])
                    best_pairs(tile + 1, GATHERED + 1, tile, [])
                dve.wait_ge(av_done, (tile + 1) * HEADS)
                v.reciprocal(prob_inv[:, :], prob_sum[:, :])
                done()
                v.tensor_tensor(attended[:, :].rearrange("p (h d) -> p h d", d=D),
                                bank[6][:, :].rearrange("p (h d) -> p h d", d=D),
                                over(prob_inv[:, :], [P, HEADS, D]), ALU.mult).then_inc(av_scaled, 1)
                if not last:
                    mark_pairs(tile + 1, GATHERED + 1, tile, [])
                dve.wait_ge(y_done, tile + 1)
                dve.wait_ge(y_free, tile + 1)
                v.tensor_tensor(y[:, :], bank[4][:, 0:D], h[:, bass.ds(tile, 1), :].rearrange("p a d -> p (a d)"),
                                ALU.add).then_inc(y_ready, 1)
            for r in range(ROUNDS):
                tile_step(r * PER_ROUND, False, None)
                for lo, hi in BATCH_RUNS[r]:
                    with nc.Fori(lo, hi, engines=[dve.engine]) as b:
                        tile_step(r * PER_ROUND + 1 + b, True, b)
                    if (r, hi) == NEXT_FRONT:
                        next_front(r + 1)
            tile_step(TILES - 1, True, GROUP - 1, last=True)


def kernel(**inputs):
    import numpy as np
    import concourse.bacc as bacc
    from concourse import mybir as _mybir
    from concourse.bass_utils import run_bass_kernel_spmd as run

    a = {k: np.asarray(t) for k, t in inputs.items()}

    x = a["x"].reshape(BATCH, 3, 4, 16, 4, 16).transpose(1, 3, 5, 0, 2, 4).reshape(KPATCH, P, ROUNDS * P)
    tables = np.zeros((EMB, VCHUNKS * P), np.float32)
    for i, (name, at) in enumerate([("et", 0), ("fc", 64), ("sc", 128), ("of", 256), ("tt", 384), ("rc", 448)]):
        e = a["L0_txt_E_" + name]
        tables[16 * i:16 * (i + 1), at:at + e.shape[0]] = e.T
    arrays = {
        "patches": x.transpose(1, 0, 2),
        "tok_w": a["L0_tok_W"].T.reshape(KPATCH, P, D).transpose(1, 0, 2),
        "tok_b": a["L0_tok_b"].reshape(1, D),
        "tokens": np.stack([a[n].reshape(-1) for n in ("x_txt", "itok_BS_0_255", "itok_BS_0_511", "itok_BS_0_127",
                                                       "itok_BS_0_63", "itok_BS_0_3")]),
        "tables": tables.reshape(EMB, VCHUNKS, P),
        "txt_w": a["L0_txt_W"].T,
        "vectors": np.concatenate([a[n].reshape(-1) for n in (
            "L0_txt_b", "L0_txt_gamma", "L0_txt_beta", "L0_attn_kln_weight", "L0_attn_kln_bias",
            "L0_attn_vln_weight", "L0_attn_vln_bias")]).reshape(1, 7 * D),
        "pk_w": a["L0_ffn_Wq_pk"].reshape(D, 2, HEADS, KD).transpose(3, 2, 1, 0).reshape(KD, 2 * HEADS, D),
        "pk_keys": a["L0_ffn_pk_keys"].transpose(3, 2, 0, 1).reshape(KD, 2 * HEADS, NK),
        "q_w": a["L0_ffn_Wq"],
        "kv_table": np.concatenate([a["L0_ffn_keys_table"], a["L0_ffn_values_table"]], axis=1),
        "o_w": a["L0_ffn_Wo"].reshape(4, P, D).transpose(1, 0, 2),
    }
    arrays = {k: np.ascontiguousarray(t) for k, t in arrays.items()}
    nc = bacc.Bacc("TRN2", target_bir_lowering=False, num_devices=1)
    args = [nc.dram_tensor(k, t.shape, _mybir.dt.from_np(t.dtype), kind="ExternalInput").ap()
            for k, t in arrays.items()]
    args.append(nc.dram_tensor("out", (TILES * P, D), _mybir.dt.float32, kind="ExternalOutput").ap())
    build(nc, *args)
    tiles = run(nc, [arrays], core_ids=[0]).results[0]["out"].reshape(ROUNDS, PER_ROUND, P, D)
    patch = tiles[:, 0].reshape(BATCH, PATCHES, D)
    text = tiles[:, 1:].reshape(BATCH, P, D)
    return np.concatenate([patch, text], axis=1)
```
